# Optimizing a Trainium2 kernel written in Bass

```python
import numpy as np
import jax
import jax.numpy as jnp

def _softmax(x, axis=-1):
    return jax.nn.softmax(x, axis=axis)

def _gelu(x):
    return jax.nn.gelu(x, approximate=True)

def _silu(x):
    return jax.nn.silu(x)

def _sigmoid(x):
    return jax.nn.sigmoid(x)

def _layernorm(x, axis=-1, eps=1e-05):
    m = jnp.mean(x, axis=axis, keepdims=True)
    v = jnp.var(x, axis=axis, keepdims=True)
    return (x - m) / jnp.sqrt(v + eps)

def _scatter_add(tgt, idx, src, axis=0):
    return tgt.at[idx].add(src)

def _segment_sum(src, seg, n):
    return jax.ops.segment_sum(src, seg, n)
kernel_name = 'mk_flamingo_gated_d1_seqx_r8_fc4309'

def setup_inputs(seed: int=0):
    np.random.seed(seed)
    _w = jnp.asarray

    def _rec_inputs():
        import jax
        import jax.numpy as jnp
        _rk = jax.random.key(seed)
        x = 7.22e-05 + 1 * jax.random.normal(jax.random.fold_in(_rk, 1), (4, 256, 256), jnp.float32)
        _lenS = 256 - jax.random.randint(jax.random.fold_in(_rk, 7), (4,), 0, max(1, 256 // 4) + 1, jnp.int32)
        _lenS2 = 256 - jax.random.randint(jax.random.fold_in(_rk, 8), (4,), 0, max(1, 256 // 4) + 1, jnp.int32)
        _ctx_1024P = jax.random.normal(jax.random.fold_in(_rk, 11), (4, 16, 128), jnp.float32)
        _ctx_1024c = jax.random.dirichlet(jax.random.fold_in(_rk, 511), 0.3 * jnp.ones((16,), jnp.float32), (4, 256))
        _ctx_1024t = jnp.einsum('bsk,bkd->bsd', _ctx_1024c, _ctx_1024P)
        _ctx_1024t = _ctx_1024t * jax.lax.rsqrt(jnp.mean(jnp.square(_ctx_1024t)) + 1e-12) * 0.953939
        ctx_1024 = 2.81802e-05 + 1.00001 * (_ctx_1024t + 0.3 * jax.random.normal(jax.random.fold_in(_rk, 611), (4, 256, 128), jnp.float32))
        _g = jax.random.normal(jax.random.fold_in(_rk, 9001), (2, 1), jnp.float32)
        _g = jnp.sign(_g) * jnp.maximum(jnp.abs(_g), 1.0) + (_g == 0) * 1.0
        g_xattn = _g[0]
        g_ffn = _g[1]
        return (x, ctx_1024, g_xattn, g_ffn)
    x, ctx_1024, g_xattn, g_ffn = _rec_inputs()

    def _L0_xattn_setup():
        import jax, jax.numpy as jnp
        import numpy as np
        key = jax.random.key(seed)
        ks = jax.random.split(key, 6)
        B, L, N, C, D = (8, 64, 256, 128, 128)
        return {'teacher_logits': jax.random.normal(ks[0], (B, L, N), dtype=jnp.float32), 'teacher_features': jax.random.normal(ks[1], (B, N, C), dtype=jnp.float32), 'Wq': jax.random.normal(ks[2], (D, C), dtype=jnp.float32) * (1.0 / np.sqrt(C)), 'bq': jnp.zeros((D,), dtype=jnp.float32), 'Wk': jax.random.normal(ks[3], (D, C), dtype=jnp.float32) * (1.0 / np.sqrt(C)), 'bk': jnp.zeros((D,), dtype=jnp.float32)}
    _L0_xattn_all = _L0_xattn_setup()
    _L0_xattn_in = {k: v for k, v in _L0_xattn_all.items() if k in ('Wq', 'bq', 'Wk', 'bk')}
    del _L0_xattn_all

    def _L0_ffn_setup():
        import jax, jax.numpy as jnp
        import numpy as np
        TOP_K = 8
        NEG_INF = -1000000000.0
        key = jax.random.key(seed)
        ks = jax.random.split(key, 6)
        B, S, H, I, E, G, GS = (1, 256, 256, 176, 64, 8, 8)
        sc = 0.02
        return {'hidden_states': jax.random.normal(ks[0], (B, S, H), jnp.float32), 'gate_w': jax.random.normal(ks[1], (E, H), jnp.float32) * sc, 'mask_up_w': jax.random.normal(ks[2], (G, H, GS), jnp.float32) * sc, 'gate_proj_w': jax.random.normal(ks[3], (G, I, H), jnp.float32) * sc, 'up_proj_w': jax.random.normal(ks[4], (G, I, H), jnp.float32) * sc, 'down_proj_w': jax.random.normal(ks[5], (G, H, I), jnp.float32) * sc, 'inv_map': jnp.arange(G * GS, dtype=jnp.int64).reshape(G, GS)}
    _L0_ffn_all = _L0_ffn_setup()
    _L0_ffn_in = {k: v for k, v in _L0_ffn_all.items() if k in ('gate_w', 'mask_up_w', 'gate_proj_w', 'up_proj_w', 'down_proj_w', 'inv_map')}
    del _L0_ffn_all
    return {'x': x, 'ctx_1024': ctx_1024, 'g_xattn': g_xattn, 'g_ffn': g_ffn, 'L0_xattn_Wq': _L0_xattn_in['Wq'], 'L0_xattn_bq': _L0_xattn_in['bq'], 'L0_xattn_Wk': _L0_xattn_in['Wk'], 'L0_xattn_bk': _L0_xattn_in['bk'], 'L0_ffn_gate_w': _L0_ffn_in['gate_w'], 'L0_ffn_mask_up_w': _L0_ffn_in['mask_up_w'], 'L0_ffn_gate_proj_w': _L0_ffn_in['gate_proj_w'], 'L0_ffn_up_proj_w': _L0_ffn_in['up_proj_w'], 'L0_ffn_down_proj_w': _L0_ffn_in['down_proj_w'], 'L0_ffn_inv_map': _L0_ffn_in['inv_map']}

def reference(x, ctx_1024, g_xattn, g_ffn, L0_xattn_Wq, L0_xattn_bq, L0_xattn_Wk, L0_xattn_bk, L0_ffn_gate_w, L0_ffn_mask_up_w, L0_ffn_gate_proj_w, L0_ffn_up_proj_w, L0_ffn_down_proj_w, L0_ffn_inv_map):
    import jax
    import jax.numpy as jnp

    def _L0_xattn_ref(teacher_logits, teacher_features, Wq, bq, Wk, bk):
        import jax, jax.numpy as jnp
        import numpy as np
        query = jnp.einsum('bnc,dc->bnd', teacher_features, Wq) + bq
        key = jnp.einsum('bnc,dc->bnd', teacher_features, Wk) + bk
        energy = jnp.einsum('bnd,bmd->bnm', query, key)
        attention = jax.nn.softmax(energy, axis=-1)
        x_m = jnp.einsum('bln,bmn->blm', teacher_logits, attention)
        return x_m

    def _L0_ffn_ref(hidden_states, gate_w, mask_up_w, gate_proj_w, up_proj_w, down_proj_w, inv_map):
        import jax, jax.numpy as jnp
        import numpy as np
        TOP_K = 8
        NEG_INF = -1000000000.0
        B, S, H = hidden_states.shape
        x = hidden_states.reshape(-1, H)
        N = x.shape[0]
        E = gate_w.shape[0]
        scores = jax.nn.softmax(x @ gate_w.T, axis=-1)
        topk_w, topk_idx = jax.lax.top_k(scores, TOP_K)
        w_e = jnp.zeros((N, E), x.dtype).at[jnp.arange(N)[:, None], topk_idx].add(topk_w)
        flat = w_e[:, inv_map]
        scalar = flat.sum(-1)
        soft = jax.nn.softmax(jnp.where(flat == 0, NEG_INF, flat), axis=-1)
        xg = x[:, None, :] + jnp.einsum('ngi,ghi->ngh', soft, mask_up_w)
        g = jnp.einsum('ngh,gih->ngi', xg, gate_proj_w)
        u = jnp.einsum('ngh,gih->ngi', xg, up_proj_w)
        a = jax.nn.silu(g) * u
        d = jnp.einsum('ngi,ghi->ngh', a, down_proj_w)
        y = jnp.einsum('ng,ngh->nh', scalar, d)
        return y.reshape(B, S, H)
    x = x + jnp.tanh(g_xattn[0]) * _L0_xattn_ref(_layernorm(x, axis=-1), ctx_1024, L0_xattn_Wq, L0_xattn_bq, L0_xattn_Wk, L0_xattn_bk)
    x = x + jnp.tanh(g_ffn[0]) * _L0_ffn_ref(_layernorm(x, axis=-1), L0_ffn_gate_w, L0_ffn_mask_up_w, L0_ffn_gate_proj_w, L0_ffn_up_proj_w, L0_ffn_down_proj_w, L0_ffn_inv_map)
    return x

_drawn_inputs = setup_inputs


def setup_inputs(seed=0):
    import zlib

    import numpy as np

    out = dict(_drawn_inputs(seed))
    spreads = {'L0_xattn_bq': (0.0, 0.1), 'L0_xattn_bk': (0.0, 0.8)}
    factors = {'L0_ffn_gate_w': 8.0,
     'L0_ffn_mask_up_w': 8.0,
     'L0_ffn_gate_proj_w': 8.0,
     'L0_ffn_up_proj_w': 8.0,
     'L0_ffn_down_proj_w': 8.0}
    for name, (base, spread) in spreads.items():
        noise = np.random.default_rng([zlib.crc32(name.encode()), seed]).standard_normal(out[name].shape)
        drawn = base * np.exp(spread * noise) if base else spread * noise
        out[name] = jnp.asarray(drawn.astype(out[name].dtype))
    for name, factor in factors.items():
        out[name] = (out[name] * factor).astype(out[name].dtype)
    return out
```

```python
from contextlib import ExitStack

import numpy as np

import concourse.bass as bass
from concourse import mybir

ALU = mybir.AluOpType
ACT = mybir.ActivationFunctionType
AX = mybir.AxisListType
F32 = mybir.dt.float32
F16 = mybir.dt.float16
I32 = mybir.dt.int32

P = 128
B, L, D = 4, 256, 256
C = 128
E, G, GS, INNER = 64, 8, 8, 176
T = B * L // P
TB = L // P
KD = D // P
CH = 512
NCH = B * L // CH
TC = CH // P
BC = CH // L
GI = G * INNER
NJ = GI // P
SG = 5
COPY = SG * GS
BASE = (0, G - SG)
SPLIT = 6
SC_SCALE = 256.0
EPS = 1e-5
TINY = 2.0 ** -40
MAGIC = float(0x5F3759DF)


def mu_segments():
    edge = SPLIT * P
    out = []
    for g in range(G):
        a, b = g * INNER, (g + 1) * INNER
        if a < edge:
            out.append((0, g - BASE[0], a, min(b, edge)))
        if b > edge:
            out.append((1, g - BASE[1], max(a, edge), b))
    return out


K_ID, K_IND, K_NEG, K_IOTA, K_END = 0, P, P + GI, P + GI + 1, P + GI + 2


def constants():
    c = np.zeros((P, K_END), np.float32)
    c[:, K_ID:K_ID + P] = np.eye(P)
    for r in range(2 * G):
        g = r % G
        c[r, K_IND + g * INNER:K_IND + (g + 1) * INNER] = 1.0 / SC_SCALE
    c[COPY:2 * COPY, K_NEG] = -1.0
    c[:, K_IOTA] = np.arange(P)
    return c


def block_kernel(nc, ctxT, x, wqT, wkT, bq, bk, gates, gateT, upT, downT, maskT, gwT, inv_map, consts, out):
    with ExitStack() as ctx:
        def sb(name, shape, dt=F32):
            return ctx.enter_context(nc.sbuf_tensor(name, shape, dt))

        def sem(name):
            return ctx.enter_context(nc.semaphore(name))

        ctx_sb = sb("ctx_sb", [P, B * L])
        wq_sb, wk_sb = sb("wq_sb", [P, C]), sb("wk_sb", [P, C])
        bq_sb, bk_sb = sb("bq_sb", [P, 1]), sb("bk_sb", [P, 1])
        gates_sb, tg = sb("gates_sb", [P, 2]), sb("tg", [P, 2])
        cst = sb("cst", [P, K_END])
        x_sb = sb("x_sb", [P, T, D])
        w_all = sb("w_all", [P, 2 * KD * GI])
        w32 = [w_all[:, w * KD * GI:(w + 1) * KD * GI].rearrange("p (k j) -> p k j", k=KD) for w in range(2)]
        w_hi = [sb("gate_hi", [P, KD, GI], F16), sb("up_hi", [P, KD, GI], F16)]
        w_lo = [sb("gate_lo", [P, KD, GI], F16), sb("up_lo", [P, KD, GI], F16)]
        down32 = sb("down32", [P, NJ, D])
        down_hl = sb("down_hl", [P, NJ, 2, D], F16)
        mask32 = sb("mask32", [P, KD, E])
        mask_hi, mask_lo = sb("mask_hi", [P, KD, E], F16), sb("mask_lo", [P, KD, E], F16)
        pad_hi = sb("pad_hi", [P, KD, 2, SG * P], F16)
        pad_lo = sb("pad_lo", [P, KD, 2, SG * P], F16)
        mu_hi = sb("mu_hi", [P, 2, 2, INNER], F16)
        mu = sb("mu", [P, 2, GI], F16)
        gw32 = sb("gw32", [P, KD, E])
        gw_hi, gw_lo = sb("gw_hi", [P, KD, E], F16), sb("gw_lo", [P, KD, E], F16)
        inv_i, inv_f, inv_n = sb("inv_i", [E, E], I32), sb("inv_f", [E, E]), sb("inv_n", [E, E])
        onehot = sb("onehot", [E, E])
        id16 = sb("id16", [P, P], F16)
        ind16 = sb("ind16", [P, GI], F16)
        qT, kT = sb("qT", [P, B * L]), sb("kT", [P, B * L])
        xh1 = sb("xh1", [P, T, D])
        stats, mv = sb("stats", [P, TC, 6]), sb("mv", [P, T, 2])
        stats2, mv2 = sb("stats2", [P, TB, 6]), sb("mv2", [P, T, 2])
        nv, ny, nt = sb("nv", [P, T]), sb("ny", [P, T]), sb("nt", [P, T])
        nv2, ny2, nt2 = sb("nv2", [P, T]), sb("ny2", [P, T]), sb("nt2", [P, T])
        rmax, rsum, rinv = sb("rmax", [P, T]), sb("rsum", [P, T]), sb("rinv", [P, T])
        att = sb("att", [P, T, L])
        xh1T, attT = sb("xh1T", [P, 2, TB, L]), sb("attT", [P, B, TB, L])
        xh2 = xh1
        xT_hi, xT_lo = sb("xT_hi", [P, KD, B * L], F16), sb("xT_lo", [P, KD, B * L], F16)
        lmax, lsum, linv = sb("lmax", [P, T]), sb("lsum", [P, T]), sb("linv", [P, T])
        score, rest, we = sb("score", [P, T, E]), sb("rest", [P, T, E]), sb("we", [P, T, E])
        top8 = sb("top8", [P, T, 8])
        weT = sb("weT", [E, B * L])
        fexp, live = score, rest
        den, dinv, scal = sb("den", [P, T, G]), sb("dinv", [P, T, G]), sb("scal", [P, T, G])
        soft = sb("soft", [P, T, E])
        stk = sb("stk", [P, T, 2, P], F16)
        sck = sb("sck", [P, T, 2 * G], F16)
        stkT = sb("stkT", [P, 2, B * L], F16)
        sckT = sb("sckT", [P, B * L], F16)
        silu, act32 = sb("silu", [P, 2, CH]), sb("act32", [P, 2, CH])
        a_hi = w_all[:, :].bitcast(F16).rearrange("p (c n) -> p c n", c=NJ)
        a_lo = sb("a_lo", [P, NJ, B * L], F16)

        bank = [ctx.enter_context(nc.psum_tensor(f"bank{i}", [P, 512], F32)) for i in range(8)]
        WORK, XT_WORK = (0, 2, 6, 7), (1, 3, 6, 7)
        GATE, UP, SCAL = (0, 1), (2, 3), (4, 5)

        ld = {n: sem("ld_" + n) for n in ("ctx0", "ctx1", "wqk", "bqk", "gates", "cst", "x0", "x1", "mask", "gw",
                                           "inv", "gate", "up", "down")}
        s_zero, s_id16, s_ind16 = sem("zeroed"), sem("id16_ready"), sem("ind16_ready")
        s_tg = sem("gates_tanh")
        s_q, s_k, s_qc, s_kc = sem("q_ready"), sem("k_ready"), sem("q_copied"), sem("k_copied")
        s_rstd1, s_xh1 = sem("rstd1_ready"), sem("xh1_ready")
        s_e, s_rmax, s_exp, s_att = sem("energy_ready"), sem("rowmax_ready"), sem("exp_ready"), sem("att_ready")
        s_attT, s_attTc = sem("attT_ready"), sem("attT_copied")
        s_xhT, s_xhTc = sem("xh1T_ready"), sem("xh1T_copied")
        s_xm, s_x1, s_xh2 = sem("xm_ready"), sem("x1_ready"), sem("xh2_ready")
        s_x2T, s_x2hi, s_x2lo = sem("xh2T_ready"), sem("xT_hi_ready"), sem("xT_lo_ready")
        s_lg, s_lmax, s_lexp, s_we = sem("logits_ready"), sem("lmax_ready"), sem("lexp_ready"), sem("we_ready")
        s_weT, s_weTc = sem("weT_ready"), sem("weT_copied")
        s_fl, s_fexp = sem("flat_ready"), sem("fexp_ready")
        s_stk, s_stT, s_stTc = sem("stack_ready"), sem("stackT_ready"), sem("stackT_copied")
        s_onehot = sem("onehot_ready")
        s_whi = [sem("gate_hi_ready"), sem("up_hi_ready")]
        s_wlo = [sem("gate_lo_ready"), sem("up_lo_ready")]
        s_dhi, s_dlo = sem("down_hi_ready"), sem("down_lo_ready")
        s_mhi, s_mlo, s_pad = sem("mask_hi_ready"), sem("mask_lo_ready"), sem("pad_ready")
        s_gwhi, s_gwlo = sem("gw_hi_ready"), sem("gw_lo_ready")
        s_mup, s_muhi, s_mu = sem("mu_psum_ready"), sem("mu_hi_ready"), sem("mu_ready")
        s_g, s_u, s_sc = sem("g_ready"), sem("u_ready"), sem("sc_ready")
        s_silu, s_a, s_ahi, s_alo = sem("silu_ready"), sem("act_ready"), sem("a_hi_ready"), sem("a_lo_ready")
        s_prod, s_y0 = sem("silu_up_ready"), sem("y0_added")
        s_y, s_out, s_st = sem("y_ready"), sem("out_ready"), sem("stored")
        dve_step, pool_step = sem("dve_step"), sem("pool_step")

        SEG = mu_segments()
        MU_BANK = (4, 5)
        ident = cst[:, K_ID:K_ID + P]
        neg_mu = cst[:, K_NEG:K_NEG + 1]
        xv = x.rearrange("b (t p) d -> p (b t) d", p=P)
        ov = out.rearrange("b (t p) d -> p (b t) d", p=P)

        def pad_window(pad, k, s, slot):
            return pad[:, k, s, (P - GS) * slot:(P - GS) * slot + P]

        block = ctx.enter_context(nc.Block())

        @block.sync
        def _(sp):
            sp.dma_start(wq_sb[:, :], wqT).then_inc(ld["wqk"], 16)
            sp.dma_start(wk_sb[:, :], wkT).then_inc(ld["wqk"], 16)
            sp.dma_start(x_sb[:, 0:TC, :], xv[:, 0:TC, :]).then_inc(ld["x0"], 16)
            sp.dma_start(cst[:, :], consts).then_inc(ld["cst"], 16)
            sp.dma_start(mask32[:, :, :], maskT.rearrange("(k p) e -> p k e", p=P)).then_inc(ld["mask"], 16)
            sp.dma_start(gw32[:, :, :], gwT.rearrange("(k p) e -> p k e", p=P)).then_inc(ld["gw"], 16)
            sp.dma_start(w32[0][:, :, :], gateT.rearrange("(k p) j -> p k j", p=P)).then_inc(ld["gate"], 16)
            sp.dma_start(w32[1][:, :, :], upT.rearrange("(k p) j -> p k j", p=P)).then_inc(ld["up"], 16)
            sp.dma_start(ctx_sb[:, CH:], ctxT[:, CH:]).then_inc(ld["ctx1"], 16)
            sp.dma_start(x_sb[:, TC:T, :], xv[:, TC:T, :]).then_inc(ld["x1"], 16)
            sp.dma_start(down32[:, :, :], downT.rearrange("(c p) d -> p c d", p=P)).then_inc(ld["down"], 16)
            with sp.Fori(0, T) as t:
                sp.wait_ge(s_out, t + 1)
                sp.dma_start(ov[:, bass.ds(t, 1), :], x_sb[:, bass.ds(t, 1), :]).then_inc(s_st, 16)
            sp.wait_ge(s_st, 16 * T)

        @block.tensor
        def _(pe):
            def split_mm(dst, lhi, llo, rhi, rlo, start, stop):
                pe.matmul(dst, lhi, rhi, start=start, stop=False)
                pe.matmul(dst, lhi, rlo, start=False, stop=False)
                return pe.matmul(dst, llo, rhi, start=False, stop=stop)

            def project(ch, q_bank, k_bank):
                n = slice(ch * CH, (ch + 1) * CH)
                pe.matmul(bank[q_bank][:, :], wq_sb[:, :], ctx_sb[:, n], start=True, stop=True).then_inc(s_q, 1)
                pe.matmul(bank[k_bank][:, :], wk_sb[:, :], ctx_sb[:, n], start=True, stop=True).then_inc(s_k, 1)

            def energy(b):
                for t in range(TB):
                    m = b * L + t * P
                    i = pe.matmul(bank[WORK[b]][:, t * L:(t + 1) * L], qT[:, m:m + P], kT[:, b * L:(b + 1) * L],
                                  start=True, stop=True)
                i.then_inc(s_e, 1)

            def transpose_batch(b, src, dst_bank, done):
                for k in range(KD):
                    for t in range(TB):
                        i = pe.transpose(dst_bank[:, k * L + t * P:k * L + (t + 1) * P],
                                         src[:, b * TB + t, k * P:(k + 1) * P], ident)
                i.then_inc(done, 1)

            def xh1_transpose(b):
                pe.wait_ge(s_xh1, TB * (b + 1))
                transpose_batch(b, xh1, bank[XT_WORK[b]], s_xhT)

            def att_transpose(b):
                pe.wait_ge(s_att, TB * (b + 1))
                transpose_batch(b, att, bank[WORK[b]], s_attT)

            def mix(b):
                pe.wait_ge(s_attTc, b + 1)
                pe.wait_ge(s_xhTc, b + 1)
                for t in range(TB):
                    for k in range(KD):
                        i = pe.matmul(bank[WORK[b]][:, t * L:(t + 1) * L], xh1T[:, b % 2, k, t * P:(t + 1) * P],
                                      attT[:, b, k, :], start=(k == 0), stop=(k == KD - 1))
                i.then_inc(s_xm, 1)

            def xh2_transpose(b):
                pe.wait_ge(s_xh2, b + 1)
                transpose_batch(b, xh2, bank[WORK[b]], s_x2T)

            def logits(b):
                if b == 0:
                    pe.wait_ge(s_gwhi, 1)
                    pe.wait_ge(s_gwlo, 1)
                pe.wait_ge(s_x2hi, b + 1)
                pe.wait_ge(s_x2lo, b + 1)
                for t in range(TB):
                    m = slice(b * L + t * P, b * L + (t + 1) * P)
                    dst = bank[WORK[b]][:, t * E:(t + 1) * E]
                    for k in range(KD):
                        pe.matmul(dst, xT_lo[:, k, m], gw_lo[:, k, :], start=(k == 0), stop=False)
                        i = split_mm(dst, xT_hi[:, k, m], xT_lo[:, k, m], gw_hi[:, k, :], gw_lo[:, k, :],
                                     False, k == KD - 1)
                i.then_inc(s_lg, 1)

            def we_transpose(b):
                pe.wait_ge(s_we, b + 1)
                for t in range(TB):
                    i = pe.transpose(bank[WORK[b]][0:E, t * P:(t + 1) * P], we[:, b * TB + t, :], ident)
                i.then_inc(s_weT, 1)

            def gather(b):
                if b == 0:
                    pe.wait_ge(s_onehot, 1)
                pe.wait_ge(s_weTc, b + 1)
                for t in range(TB):
                    i = pe.matmul(bank[WORK[b]][:, t * E:(t + 1) * E], weT[:, b * L + t * P:b * L + (t + 1) * P],
                                  onehot[:, :], start=True, stop=True)
                i.then_inc(s_fl, 1)

            def stack_transpose(b):
                if b == 0:
                    pe.wait_ge(s_id16, 1)
                pe.wait_ge(s_stk, b + 1)
                dst = bank[WORK[b]][:, :].bitcast(F16)
                for t in range(TB):
                    for s in range(2):
                        pe.transpose(dst[:, s * L + t * P:s * L + (t + 1) * P], stk[:, b * TB + t, s, :], id16[:, :])
                    i = pe.transpose(dst[0:2 * G, 2 * L + t * P:2 * L + (t + 1) * P], sck[:, b * TB + t, :],
                                     id16[:, :])
                i.then_inc(s_stT, 1)

            def mu_segment(n):
                s, slot, a, z = SEG[n]
                if n == 0:
                    pe.wait_ge(s_pad, 2)
                    for w in range(2):
                        pe.wait_ge(s_whi[w], 1)
                        pe.wait_ge(s_wlo[w], 1)
                if n >= 2:
                    pe.wait_ge(s_mu, n - 1)
                for w in range(2):
                    dst = bank[MU_BANK[n % 2]][:, w * INNER:w * INNER + z - a]
                    for k in range(KD):
                        i = split_mm(dst, pad_window(pad_hi, k, s, slot), pad_window(pad_lo, k, s, slot),
                                     w_hi[w][:, k, a:z], w_lo[w][:, k, a:z], k == 0, k == KD - 1)
                i.then_inc(s_mup, 1)

            def unit(ch, c, s, par, used):
                n = slice(ch * CH, (ch + 1) * CH)
                col = bass.ds(c * P, P)
                for w, dst, done, freed in ((0, bank[GATE[par]], s_g, s_silu), (1, bank[UP[par]], s_u, s_a)):
                    if used is not None:
                        pe.wait_ge(freed, used)
                    for k in range(KD):
                        split_mm(dst[:, :], w_hi[w][:, k, col], w_lo[w][:, k, col],
                                 xT_hi[:, k, n], xT_lo[:, k, n], k == 0, False)
                    pe.matmul(dst[:, :], mu[:, w, col], stkT[:, s, n], start=False, stop=True).then_inc(done, 1)
                pe.matmul(bank[SCAL[par]][:, :], ind16[:, col], sckT[:, n], start=True, stop=True).then_inc(s_sc, 1)

            pe.wait_ge(ld["wqk"], 32)
            pe.wait_ge(ld["ctx0"], 16)
            project(0, 4, 5)
            pe.wait_ge(s_qc, 1)
            pe.wait_ge(s_kc, 1)
            energy(0)
            energy(1)
            pe.wait_ge(ld["cst"], 16)
            xh1_transpose(0)
            xh1_transpose(1)
            for stage in (att_transpose, mix, xh2_transpose, logits):
                for b in range(BC):
                    stage(b)
            for n in range(3):
                mu_segment(n)
            for b in range(BC):
                we_transpose(b)
            for n in range(3, 6):
                mu_segment(n)
            for b in range(BC):
                gather(b)
            for n in range(6, len(SEG)):
                mu_segment(n)
            for b in range(BC):
                stack_transpose(b)
            pe.wait_ge(s_ind16, 1)
            pe.wait_ge(s_mu, len(SEG))
            pe.wait_ge(s_stTc, 2 * BC)

            for c in range(NJ):
                unit(0, c, int(c >= SPLIT), c % 2, c - 1 if c >= 2 else None)
                if c == 0:
                    pe.wait_ge(ld["ctx1"], 16)
                    project(1, 6, 7)
                elif c == 1:
                    pe.wait_ge(s_qc, 2)
                    pe.wait_ge(s_kc, 2)
                    energy(2)
                    energy(3)
                elif c == 2:
                    pe.wait_ge(s_exp, 3 * TB)
                    xh1_transpose(2)
                    pe.wait_ge(s_exp, 4 * TB)
                    xh1_transpose(3)
                elif c == 3:
                    pe.wait_ge(s_xhTc, 3)
                    att_transpose(2)
                    pe.wait_ge(s_xhTc, 4)
                    att_transpose(3)
                else:
                    stage = {4: mix, 5: xh2_transpose, 6: logits, 7: we_transpose, 8: gather}.get(c)
                    if stage:
                        stage(2)
                        stage(3)
            stack_transpose(2)
            stack_transpose(3)
            pe.wait_ge(s_stTc, 2 * B)

            for s, first, last in ((0, 0, SPLIT // 2), (1, SPLIT // 2, NJ // 2)):
                with pe.Fori(first, last) as i:
                    for h in range(2):
                        unit(1, 2 * i + h, s, (NJ + h) % 2, NJ + 2 * i + h - 1)
            unit(1, NJ - 1, 1, (2 * NJ - 1) % 2, 2 * NJ - 2)

            def down_tile(t, h, used):
                if used is not None:
                    pe.wait_ge(s_out, used)
                tok = bass.ds(t * P, P)
                dst = bank[6 + h]
                for c in range(NJ):
                    pe.matmul(dst[:, :], a_hi[:, c, tok], down_hl[:, c, :, :].rearrange("p a d -> p (a d)"),
                              start=(c == 0), stop=False)
                    y = pe.matmul(dst[:, 0:D], a_lo[:, c, tok], down_hl[:, c, 0, :],
                                  start=False, stop=(c == NJ - 1))
                y.then_inc(s_y, 1)

            pe.wait_ge(s_dhi, 1)
            pe.wait_ge(s_dlo, 1)
            pe.wait_ge(s_ahi, NJ)
            pe.wait_ge(s_alo, NJ)
            down_tile(0, 0, None)
            down_tile(1, 1, None)
            with pe.Fori(1, TC // 2) as i:
                for h in range(2):
                    down_tile(2 * i + h, h, 2 * i + h - 1)
            pe.wait_ge(s_ahi, NCH * NJ)
            pe.wait_ge(s_alo, NCH * NJ)
            with pe.Fori(TC // 2, T // 2) as i:
                for h in range(2):
                    down_tile(2 * i + h, h, 2 * i + h - 1)

        @block.scalar
        def _(act):
            act.dma_start(ctx_sb[:, 0:CH], ctxT[:, 0:CH]).then_inc(ld["ctx0"], 16)
            act.dma_start(bq_sb[:, :], bq.rearrange("(p a) -> p a", a=1)).then_inc(ld["bqk"], 16)
            act.dma_start(bk_sb[:, :], bk.rearrange("(p a) -> p a", a=1)).then_inc(ld["bqk"], 16)
            act.dma_start(inv_i[:, :], inv_map.partition_broadcast(E)).then_inc(ld["inv"], 16)
            act.dma_start(gates_sb[:, :], gates.partition_broadcast(P)).then_inc(ld["gates"], 16)

            def q_copy(ch, q_bank):
                act.wait_ge(s_q, ch + 1)
                act.activation(qT[:, ch * CH:(ch + 1) * CH], bank[q_bank][:, :], ACT.Identity,
                               bias=bq_sb[:, 0:1]).then_inc(s_qc, 1)

            def exps(b):
                act.wait_ge(s_rmax, b + 1)
                for t in range(b * TB, (b + 1) * TB):
                    act.activation(att[:, t, :], bank[WORK[b]][:, (t % TB) * L:(t % TB + 1) * L], ACT.Exp,
                                   bias=rmax[:, t:t + 1], accum_out=rsum[:, t:t + 1]).then_inc(s_exp, 1)

            def attT_copy(b):
                act.wait_ge(s_attT, b + 1)
                act.copy(attT[:, b, :, :].rearrange("p k m -> p (k m)"), bank[WORK[b]][:, :]).then_inc(s_attTc, 1)

            def x2_hi(b):
                act.wait_ge(s_x2T, b + 1)
                act.copy(xT_hi[:, :, b * L:(b + 1) * L],
                         bank[WORK[b]][:, :].rearrange("p (k n) -> p k n", k=KD)).then_inc(s_x2hi, 1)

            def logit_exps(b):
                act.wait_ge(s_lmax, b + 1)
                for t in range(b * TB, (b + 1) * TB):
                    act.activation(score[:, t, :], bank[WORK[b]][:, (t % TB) * E:(t % TB + 1) * E], ACT.Exp,
                                   bias=lmax[:, t:t + 1], accum_out=lsum[:, t:t + 1]).then_inc(s_lexp, 1)

            def weT_copy(b):
                act.wait_ge(s_weT, b + 1)
                act.copy(weT[:, b * L:(b + 1) * L], bank[WORK[b]][0:E, 0:L]).then_inc(s_weTc, 1)

            def flat_exp(b):
                act.wait_ge(s_fl, b + 1)
                act.activation(fexp[:, b * TB:(b + 1) * TB, :].rearrange("p t e -> p (t e)"),
                               bank[WORK[b]][:, 0:TB * E], ACT.Exp).then_inc(s_fexp, 1)

            def stack_copy(b):
                act.wait_ge(s_stT, b + 1)
                src = bank[WORK[b]][:, :].bitcast(F16)
                act.copy(stkT[:, :, b * L:(b + 1) * L],
                         src[:, 0:2 * L].rearrange("p (s n) -> p s n", s=2)).then_inc(s_stTc, 1)
                if b == 0:
                    act.wait_ge(s_zero, 1)
                act.copy(sckT[0:2 * G, b * L:(b + 1) * L], src[0:2 * G, 2 * L:3 * L]).then_inc(s_stTc, 1)

            def weight_hi(w, k, last):
                i = act.copy(w_hi[w][:, k, :], w32[w][:, k, :])
                if last:
                    i.then_inc(s_whi[w], 1)

            def mu_high(n):
                s, slot, a, z = SEG[n]
                act.wait_ge(s_mup, n + 1)
                if n >= 2:
                    act.wait_ge(s_mu, n - 1)
                act.copy(mu_hi[:, n % 2, :, 0:z - a],
                         bank[MU_BANK[n % 2]][:, 0:2 * INNER].rearrange("p (w j) -> p w j", w=2)[:, :, 0:z - a]
                         ).then_inc(s_muhi, 1)

            def activate(n, c, par, tok, used):
                act.wait_ge(s_g, n + 1)
                if used is not None:
                    act.wait_ge(s_a, used)
                act.activation(silu[:, par, :], bank[GATE[par]][:, :], ACT.Silu).then_inc(s_silu, 1)
                act.wait_ge(s_a, n + 1)
                act.copy(a_hi[:, c, tok], act32[:, par, :]).then_inc(s_ahi, 1)

            act.wait_ge(ld["gates"], 16)
            act.activation(tg[:, :], gates_sb[:, :], ACT.Tanh).then_inc(s_tg, 1)
            act.wait_ge(ld["bqk"], 32)
            q_copy(0, 4)
            act.wait_ge(ld["mask"], 16)
            act.copy(mask_hi[:, :, :], mask32[:, :, :]).then_inc(s_mhi, 1)
            act.wait_ge(ld["gw"], 16)
            act.copy(gw_hi[:, :, :], gw32[:, :, :]).then_inc(s_gwhi, 1)
            exps(0)
            exps(1)
            act.wait_ge(ld["gate"], 16)
            weight_hi(0, 0, False)
            attT_copy(0)
            attT_copy(1)
            weight_hi(0, 1, True)
            act.wait_ge(ld["up"], 16)
            weight_hi(1, 0, False)
            x2_hi(0)
            x2_hi(1)
            weight_hi(1, 1, True)
            logit_exps(0)
            logit_exps(1)
            for n in range(3):
                mu_high(n)
            weT_copy(0)
            weT_copy(1)
            for n in range(3, 6):
                mu_high(n)
            flat_exp(0)
            flat_exp(1)
            for n in range(6, len(SEG)):
                mu_high(n)
            stack_copy(0)
            stack_copy(1)
            act.wait_ge(ld["down"], 16)
            act.copy(down_hl[:, :, 0, :], down32[:, :, :]).then_inc(s_dhi, 1)
            for c in range(NJ):
                activate(c, c, c % 2, slice(0, CH), c - 1 if c >= 2 else None)
                if c == 0:
                    q_copy(1, 6)
                stage = {1: exps, 3: attT_copy, 5: x2_hi, 6: logit_exps, 7: weT_copy, 8: flat_exp}.get(c)
                if stage:
                    stage(2)
                    stage(3)
            stack_copy(2)
            stack_copy(3)
            tok1 = slice(CH, 2 * CH)
            with act.Fori(0, NJ // 2) as i:
                for h in range(2):
                    n = 2 * i + (NJ + h)
                    activate(n, bass.ds(2 * i + h, 1), (NJ + h) % 2, tok1, n - 1)
            activate(2 * NJ - 1, NJ - 1, (2 * NJ - 1) % 2, tok1, 2 * NJ - 2)

        @block.gpsimd
        def _(pool):
            pool.memset(pad_hi[:, :, :, :], 0.0).then_inc(pool_step, 1)
            pool.memset(pad_lo[:, :, :, :], 0.0).then_inc(pool_step, 1)
            pool.memset(stk[:, :, :, :], 0.0).then_inc(s_zero, 1)
            pool.memset(sckT[:, :], 0.0).then_inc(s_zero, 1)

            def normalise1(ch):
                pool.wait_ge(s_rstd1, ch + 1)
                for t in range(ch * TC, (ch + 1) * TC):
                    pool.tensor_scalar(xh1[:, t, :], x_sb[:, t, :], mv[:, t, 0:1], ny[:, t:t + 1],
                                       ALU.subtract, ALU.mult).then_inc(s_xh1, 1)

            def activation_low(n, c, par, tok):
                pool.wait_ge(s_ahi, n + 1)
                pool.tensor_tensor(a_lo[:, c, tok], act32[:, par, :], a_hi[:, c, tok],
                                   ALU.subtract).then_inc(s_alo, 1)

            normalise1(0)
            pool.wait_ge(ld["mask"], 16)
            pool.wait_ge(s_mhi, 1)
            pool.tensor_tensor(mask_lo[:, :, :], mask32[:, :, :], mask_hi[:, :, :], ALU.subtract).then_inc(s_mlo, 1)
            pool.wait_ge(ld["gw"], 16)
            pool.wait_ge(s_gwhi, 1)
            pool.tensor_tensor(gw_lo[:, :, :], gw32[:, :, :], gw_hi[:, :, :], ALU.subtract).then_inc(s_gwlo, 1)
            pool.wait_ge(s_mlo, 1)
            pool.wait_ge(pool_step, 2)
            for pad, mask in ((pad_hi, mask_hi), (pad_lo, mask_lo)):
                for s, first in ((0, 0), (1, 1)):
                    for r in range(3):
                        for k in range(KD):
                            dst = pad[:, k, s, :].rearrange("p (g w) -> p g w", w=P)[:, first:SG, r * COPY:r * COPY + GS]
                            g0 = BASE[s] + first
                            i = pool.tensor_copy(dst, mask[:, k, g0 * GS:(g0 + SG - first) * GS]
                                                 .rearrange("p (g i) -> p g i", i=GS))
                i.then_inc(s_pad, 1)
            pool.wait_ge(ld["cst"], 16)
            pool.tensor_copy(id16[:, :], ident).then_inc(s_id16, 1)
            pool.tensor_copy(ind16[:, :], cst[:, K_IND:K_IND + GI]).then_inc(s_ind16, 1)
            pool.wait_ge(ld["up"], 16)
            pool.wait_ge(s_whi[1], 1)
            pool.tensor_tensor(w_lo[1][:, :, :], w32[1][:, :, :], w_hi[1][:, :, :], ALU.subtract).then_inc(s_wlo[1], 1)
            pool.wait_ge(ld["down"], 16)
            pool.wait_ge(s_dhi, 1)
            pool.tensor_tensor(down_hl[:, :, 1, :], down32[:, :, :], down_hl[:, :, 0, :],
                               ALU.subtract).then_inc(s_dlo, 1)
            for c in range(NJ):
                activation_low(c, c, c % 2, slice(0, CH))
                if c == 0:
                    normalise1(1)
            tok1 = slice(CH, 2 * CH)
            with pool.Fori(0, NJ // 2) as i:
                for h in range(2):
                    activation_low(2 * i + (NJ + h), bass.ds(2 * i + h, 1), (NJ + h) % 2, tok1)
            activation_low(2 * NJ - 1, NJ - 1, (2 * NJ - 1) % 2, tok1)

        @block.vector
        def _(dve):
            steps = [0]

            def step(instruction):
                steps[0] += 1
                instruction.then_inc(dve_step, 1)
                dve.wait_ge(dve_step, steps[0])

            def rsqrt(v, y, t, var, a, z, done):
                v, y, t = v[:, a:z], y[:, a:z], t[:, a:z]
                step(dve.tensor_scalar(v, var, EPS, None, ALU.add))
                step(dve.tensor_scalar(y.bitcast(I32), v.bitcast(I32), 1, None, ALU.logical_shift_right))
                step(dve.tensor_scalar(y.bitcast(I32), y.bitcast(I32), -1.0, MAGIC, ALU.mult, ALU.add))
                for n in range(3):
                    step(dve.scalar_tensor_tensor(t, y, -0.5, y, ALU.mult, ALU.mult))
                    step(dve.tensor_tensor(t, t, v, ALU.mult))
                    i = dve.scalar_tensor_tensor(y, t, 1.5, y, ALU.add, ALU.mult)
                    if n < 2 or done is None:
                        step(i)
                    else:
                        i.then_inc(done, 1)

            def statistics1(ch):
                dve.wait_ge(ld[f"x{ch}"], 16)
                for t in range(TC):
                    i = dve.bn_stats(stats[:, t, :], x_sb[:, ch * TC + t, :])
                step(i)
                for t in range(TC):
                    i = dve.bn_aggr(mv[:, ch * TC + t, :], stats[:, t, :])
                step(i)
                rsqrt(nv, ny, nt, mv[:, ch * TC:(ch + 1) * TC, 1], ch * TC, (ch + 1) * TC, s_rstd1)

            def k_copy(ch, k_bank):
                dve.wait_ge(s_k, ch + 1)
                dve.tensor_scalar(kT[:, ch * CH:(ch + 1) * CH], bank[k_bank][:, :], bk_sb[:, 0:1], None,
                                  ALU.add).then_inc(s_kc, 1)

            def row_max(b):
                dve.wait_ge(s_e, b + 1)
                dve.tensor_reduce(rmax[:, b * TB:(b + 1) * TB],
                                  bank[WORK[b]][:, :].rearrange("p (t n) -> p t n", t=TB), AX.X, ALU.max,
                                  negate=True).then_inc(s_rmax, 1)

            def scale_att(b):
                dve.wait_ge(s_exp, (b + 1) * TB)
                step(dve.reciprocal(rinv[:, b * TB:(b + 1) * TB], rsum[:, b * TB:(b + 1) * TB]))
                for t in range(b * TB, (b + 1) * TB):
                    dve.tensor_scalar(att[:, t, :], att[:, t, :], rinv[:, t:t + 1], tg[:, 0:1],
                                      ALU.mult, ALU.mult).then_inc(s_att, 1)

            def xh1T_copy(b):
                dve.wait_ge(s_xhT, b + 1)
                dve.tensor_copy(xh1T[:, b % 2, :, :].rearrange("p k n -> p (k n)"), bank[XT_WORK[b]][:, :]
                                ).then_inc(s_xhTc, 1)

            def residual_and_norm(b):
                r = slice(b * TB, (b + 1) * TB)
                dve.wait_ge(s_xm, b + 1)
                step(dve.tensor_tensor(x_sb[:, r, :].rearrange("p t d -> p (t d)"), bank[WORK[b]][:, :],
                                       x_sb[:, r, :].rearrange("p t d -> p (t d)"), ALU.add))
                for t in range(TB):
                    i = dve.bn_stats(stats2[:, t, :], x_sb[:, b * TB + t, :])
                step(i)
                for t in range(TB):
                    i = dve.bn_aggr(mv2[:, b * TB + t, :], stats2[:, t, :])
                step(i)
                rsqrt(nv2, ny2, nt2, mv2[:, r, 1], b * TB, (b + 1) * TB, None)
                for t in range(b * TB, (b + 1) * TB):
                    i = dve.tensor_scalar(xh2[:, t, :], x_sb[:, t, :], mv2[:, t, 0:1], ny2[:, t:t + 1],
                                          ALU.subtract, ALU.mult)
                i.then_inc(s_xh2, 1)

            def x2_lo(b):
                dve.wait_ge(s_x2hi, b + 1)
                dve.tensor_tensor(xT_lo[:, :, b * L:(b + 1) * L],
                                  bank[WORK[b]][:, :].rearrange("p (k n) -> p k n", k=KD),
                                  xT_hi[:, :, b * L:(b + 1) * L], ALU.subtract).then_inc(s_x2lo, 1)

            def logit_max(b):
                dve.wait_ge(s_lg, b + 1)
                dve.tensor_reduce(lmax[:, b * TB:(b + 1) * TB],
                                  bank[WORK[b]][:, 0:TB * E].rearrange("p (t e) -> p t e", t=TB), AX.X, ALU.max,
                                  negate=True).then_inc(s_lmax, 1)

            def top_scores(b):
                r = range(b * TB, (b + 1) * TB)
                dve.wait_ge(s_lexp, (b + 1) * TB)
                step(dve.reciprocal(linv[:, r[0]:r[-1] + 1], lsum[:, r[0]:r[-1] + 1]))
                for t in r:
                    i = dve.tensor_scalar(score[:, t, :], score[:, t, :], linv[:, t:t + 1], None, ALU.mult)
                step(i)
                for t in r:
                    i = dve.max(top8[:, t, :], score[:, t, :])
                step(i)
                for t in r:
                    i = dve.match_replace(rest[:, t, :], top8[:, t, :], score[:, t, :], 0.0)
                step(i)
                dve.tensor_tensor(we[:, r[0]:r[-1] + 1, :], score[:, r[0]:r[-1] + 1, :], rest[:, r[0]:r[-1] + 1, :],
                                  ALU.subtract).then_inc(s_we, 1)

            def slot_softmax(b):
                r = slice(b * TB, (b + 1) * TB)
                flat = bank[WORK[b]][:, 0:TB * E]
                dve.wait_ge(s_fexp, b + 1)
                dve.tensor_scalar(live[:, r, :].rearrange("p t e -> p (t e)"), flat, 0.0, TINY,
                                  ALU.not_equal, ALU.max)
                step(dve.tensor_reduce(scal[:, r, :].rearrange("p t g -> p (t g)"),
                                       flat.rearrange("p (g i) -> p g i", i=GS), AX.X, ALU.add))
                step(dve.tensor_tensor(fexp[:, r, :], fexp[:, r, :], live[:, r, :], ALU.mult))
                step(dve.tensor_reduce(den[:, r, :].rearrange("p t g -> p (t g)"),
                                       fexp[:, r, :].rearrange("p t (g i) -> p (t g) i", i=GS), AX.X, ALU.add))
                step(dve.reciprocal(dinv[:, r, :], den[:, r, :]))
                step(dve.tensor_tensor(soft[:, r, :].rearrange("p t (g i) -> p (t g) i", i=GS),
                                       fexp[:, r, :].rearrange("p t (g i) -> p (t g) i", i=GS),
                                       dinv[:, r, :].rearrange("p t (g a) -> p (t g) a", a=1)
                                       .to_broadcast([P, TB * G, GS]), ALU.mult))
                if b == 0:
                    dve.wait_ge(s_zero, 1)
                for s in range(2):
                    src = soft[:, r, BASE[s] * GS:BASE[s] * GS + COPY]
                    dve.tensor_copy(stk[:, r, s, 0:COPY], src)
                    i = dve.tensor_copy(stk[:, r, s, COPY:2 * COPY], src)
                step(dve.tensor_scalar(sck[:, r, 0:G], scal[:, r, :], SC_SCALE, None, ALU.mult))
                for s in range(2):
                    src = soft[:, r, BASE[s] * GS:BASE[s] * GS + COPY]
                    dve.tensor_tensor(stk[:, r, s, 2 * COPY:3 * COPY], src, stk[:, r, s, 0:COPY], ALU.subtract)
                dve.scalar_tensor_tensor(sck[:, r, G:2 * G], scal[:, r, :], SC_SCALE, sck[:, r, 0:G],
                                         ALU.mult, ALU.subtract).then_inc(s_stk, 1)

            def mu_stack(n):
                s, slot, a, z = SEG[n]
                dve.wait_ge(s_muhi, n + 1)
                dve.scalar_tensor_tensor(mu[:, :, a:z], mu_hi[:, n % 2, :, 0:z - a], neg_mu,
                                         bank[MU_BANK[n % 2]][:, 0:2 * INNER]
                                         .rearrange("p (w j) -> p w j", w=2)[:, :, 0:z - a],
                                         ALU.mult, ALU.add).then_inc(s_mu, 1)

            def multiply(n, par, low):
                dve.wait_ge(s_silu, n + 1)
                dve.wait_ge(s_u, n + 1)
                dve.tensor_tensor(silu[:, par, :], silu[:, par, :], bank[UP[par]][:, :], ALU.mult
                                  ).then_inc(s_prod, 1)
                dve.wait_ge(s_prod, n + 1)
                dve.wait_ge(s_sc, n + 1)
                if low is not None:
                    dve.wait_ge(s_ahi, low)
                    dve.wait_ge(s_alo, low)
                dve.tensor_tensor(act32[:, par, :], silu[:, par, :], bank[SCAL[par]][:, :], ALU.mult
                                  ).then_inc(s_a, 1)

            statistics1(0)
            dve.wait_ge(ld["bqk"], 32)
            k_copy(0, 5)
            dve.wait_ge(ld["inv"], 16)
            step(dve.tensor_copy(inv_f[:, :], inv_i[:, :]))
            step(dve.tensor_scalar(inv_n[:, :], inv_f[:, :], 0.0, float(E), ALU.is_lt, ALU.mult))
            step(dve.tensor_tensor(inv_f[:, :], inv_f[:, :], inv_n[:, :], ALU.add))
            step(dve.tensor_scalar(inv_f[:, :], inv_f[:, :], 0.0, float(E - 1), ALU.max, ALU.min))
            row_max(0)
            row_max(1)
            dve.wait_ge(ld["cst"], 16)
            dve.tensor_scalar(onehot[:, :], inv_f[:, :], cst[0:E, K_IOTA:K_IOTA + 1], None,
                              ALU.is_equal).then_inc(s_onehot, 1)
            dve.wait_ge(s_tg, 1)
            scale_att(0)
            scale_att(1)
            xh1T_copy(0)
            xh1T_copy(1)
            residual_and_norm(0)
            residual_and_norm(1)
            x2_lo(0)
            x2_lo(1)
            logit_max(0)
            logit_max(1)
            dve.wait_ge(ld["gate"], 16)
            dve.wait_ge(s_whi[0], 1)
            dve.tensor_tensor(w_lo[0][:, :, :], w32[0][:, :, :], w_hi[0][:, :, :], ALU.subtract
                              ).then_inc(s_wlo[0], 1)
            top_scores(0)
            top_scores(1)
            for n in range(6):
                mu_stack(n)
            slot_softmax(0)
            slot_softmax(1)
            for n in range(6, len(SEG)):
                mu_stack(n)
            for c in range(NJ):
                multiply(c, c % 2, c - 1 if c >= 2 else None)
                if c == 0:
                    statistics1(1)
                    k_copy(1, 7)
                stages = {1: (row_max,), 2: (scale_att, xh1T_copy), 4: (residual_and_norm,), 5: (x2_lo,),
                          6: (logit_max, top_scores), 8: (slot_softmax,)}.get(c, ())
                for stage in stages:
                    stage(2)
                    stage(3)
            with dve.Fori(0, NJ // 2) as i:
                for h in range(2):
                    n = 2 * i + (NJ + h)
                    multiply(n, (NJ + h) % 2, n - 1)
            multiply(2 * NJ - 1, (2 * NJ - 1) % 2, 2 * NJ - 2)

            with dve.Fori(0, T // 2) as i:
                for h in range(2):
                    t = 2 * i + h
                    row = x_sb[:, bass.ds(t, 1), :].rearrange("p t d -> p (t d)")
                    dve.wait_ge(s_y, t + 1)
                    dve.scalar_tensor_tensor(row, bank[6 + h][:, 0:D], tg[:, 1:2], row,
                                             ALU.mult, ALU.add).then_inc(s_y0, 1)
                    dve.wait_ge(s_y0, t + 1)
                    dve.scalar_tensor_tensor(row, bank[6 + h][:, D:2 * D], tg[:, 1:2], row,
                                             ALU.mult, ALU.add).then_inc(s_out, 1)


_OUT = ((B, L, D), "float32")


def kernel(x, ctx_1024, g_xattn, g_ffn, L0_xattn_Wq, L0_xattn_bq, L0_xattn_Wk, L0_xattn_bk, L0_ffn_gate_w,
           L0_ffn_mask_up_w, L0_ffn_gate_proj_w, L0_ffn_up_proj_w, L0_ffn_down_proj_w, L0_ffn_inv_map):
    import concourse.bacc as bacc
    from concourse.bass_utils import run_bass_kernel_spmd

    inv = np.ascontiguousarray(L0_ffn_inv_map).reshape(-1)
    if inv.dtype.itemsize == 8:
        inv = inv.view(np.int32)[::2]
    arrays = {
        "ctxT": np.asarray(ctx_1024).reshape(B * L, C).T,
        "x": np.asarray(x),
        "wqT": np.asarray(L0_xattn_Wq).T,
        "wkT": np.asarray(L0_xattn_Wk).T,
        "bq": np.asarray(L0_xattn_bq),
        "bk": np.asarray(L0_xattn_bk),
        "gates": np.concatenate([np.asarray(g_xattn), np.asarray(g_ffn)]),
        "gateT": np.asarray(L0_ffn_gate_proj_w).reshape(GI, D).T,
        "upT": np.asarray(L0_ffn_up_proj_w).reshape(GI, D).T,
        "downT": np.asarray(L0_ffn_down_proj_w).transpose(0, 2, 1).reshape(GI, D),
        "maskT": np.asarray(L0_ffn_mask_up_w).transpose(1, 0, 2).reshape(D, E),
        "gwT": np.asarray(L0_ffn_gate_w).T,
        "inv_map": inv,
        "consts": constants(),
    }
    arrays = {f"in_{k}": np.ascontiguousarray(v) for k, v in arrays.items()}
    nc = bacc.Bacc("TRN2", target_bir_lowering=False, num_devices=1)
    args = [nc.dram_tensor(k, v.shape, mybir.dt.from_np(v.dtype), kind="ExternalInput").ap()
            for k, v in arrays.items()]
    out = nc.dram_tensor("out", _OUT[0], mybir.dt.from_np(np.dtype(_OUT[1])), kind="ExternalOutput").ap()
    block_kernel(nc, *args, out)
    r = run_bass_kernel_spmd(nc, [arrays], core_ids=[0])
    return r.results[0]["out"]
```

```python
from contextlib import ExitStack

import numpy as np

import concourse.bass as bass
from concourse import mybir

ALU = mybir.AluOpType
ACT = mybir.ActivationFunctionType
AX = mybir.AxisListType
F32 = mybir.dt.float32
F16 = mybir.dt.float16
I32 = mybir.dt.int32

P = 128
B, L, D = 4, 256, 256
C = 128
E, G, GS, INNER = 64, 8, 8, 176
T = B * L // P
TB = L // P
KD = D // P
CH = 512
NCH = B * L // CH
TC = CH // P
BC = CH // L
GI = G * INNER
NJ = GI // P
SG = 5
COPY = SG * GS
BASE = (0, G - SG)
SPLIT = 6
SC_SCALE = 256.0
EPS = 1e-5
TINY = 2.0 ** -40
EDGE = SPLIT * P


def mu_segments():
    out = []
    for g in range(G):
        a, b = g * INNER, (g + 1) * INNER
        if a < EDGE:
            out.append((0, g - BASE[0], a, min(b, EDGE)))
        if b > EDGE:
            out.append((1, g - BASE[1], max(a, EDGE), b))
    return out


K_ID, K_NEG, K_IOTA, K_END = 0, P, P + 1, P + 2


def constants():
    c = np.zeros((P, K_END), np.float32)
    c[:, K_ID:K_ID + P] = np.eye(P)
    c[COPY:2 * COPY, K_NEG] = -1.0
    c[:, K_IOTA] = np.arange(P)
    return c


def indicator():
    c = np.zeros((2 * G, GI), np.float32)
    for r in range(2 * G):
        c[r, r % G * INNER:(r % G + 1) * INNER] = 1.0 / SC_SCALE
    return c


def block_kernel(nc, ctxT, x, wqkT, bqk, gates, gateT, upT, downT, maskgwT, inv_map, consts, ind, out):
    with ExitStack() as ctx:
        def sb(name, shape, dt=F32):
            return ctx.enter_context(nc.sbuf_tensor(name, shape, dt))

        def sem(name):
            return ctx.enter_context(nc.semaphore(name))

        ctx_sb = sb("ctx_sb", [P, B * L])
        wqk_sb, bqk_sb = sb("wqk_sb", [P, 2, C]), sb("bqk_sb", [P, 2])
        gates_sb, tg = sb("gates_sb", [P, 2]), sb("tg", [P, 2])
        cst = sb("cst", [P, K_END])
        x_sb = sb("x_sb", [P, T, D])
        w_all = sb("w_all", [P, 2 * KD * GI])
        w32 = [w_all[:, w * KD * GI:(w + 1) * KD * GI].rearrange("p (k j) -> p k j", k=KD) for w in range(2)]
        w_hi = [sb("gate_hi", [P, KD, GI], F16), sb("up_hi", [P, KD, GI], F16)]
        w_lo = [sb("gate_lo", [P, KD, GI], F16), sb("up_lo", [P, KD, GI], F16)]
        down32 = sb("down32", [P, NJ, D])
        down_hl = sb("down_hl", [P, NJ, 2, D], F16)
        mg32 = sb("mg32", [P, KD, 2 * E])
        mg_hi, mg_lo = sb("mg_hi", [P, KD, 2 * E], F16), sb("mg_lo", [P, KD, 2 * E], F16)
        mask_hi, mask_lo, gw_hi, gw_lo = mg_hi[:, :, 0:E], mg_lo[:, :, 0:E], mg_hi[:, :, E:], mg_lo[:, :, E:]
        pad_hi = sb("pad_hi", [P, KD, 2, SG * P], F16)
        pad_lo = sb("pad_lo", [P, KD, 2, SG * P], F16)
        mu_hi = sb("mu_hi", [P, 2, 2, INNER], F16)
        mu = sb("mu", [P, 2, GI], F16)
        inv_i, inv_f, inv_n = sb("inv_i", [E, E], I32), sb("inv_f", [E, E]), sb("inv_n", [E, E])
        onehot = sb("onehot", [E, E])
        id16 = sb("id16", [P, P], F16)
        ind32, ind16 = sb("ind32", [2 * G, GI]), sb("ind16", [P, GI], F16)
        qT, kT = sb("qT", [P, B * L]), sb("kT", [P, B * L])
        xh1 = sb("xh1", [P, T, D])
        stats, mv = sb("stats", [P, TC, 6]), sb("mv", [P, T, 2])
        stats2, mv2 = sb("stats2", [P, TC, 6]), sb("mv2", [P, T, 2])
        half = sb("half", [P, TC])
        var1, rstd1 = sb("var1", [P, T]), sb("rstd1", [P, T])
        var2, rstd2 = sb("var2", [P, T]), sb("rstd2", [P, T])
        rmax, rsum, rinv = sb("rmax", [P, T]), sb("rsum", [P, T]), sb("rinv", [P, T])
        att = sb("att", [P, T, L])
        xh1T, attT = sb("xh1T", [P, 2, TB, L]), sb("attT", [P, B, TB, L])
        xh2 = xh1
        xT_hi, xT_lo = sb("xT_hi", [P, KD, B * L], F16), sb("xT_lo", [P, KD, B * L], F16)
        lmax, lsum, linv = sb("lmax", [P, T]), sb("lsum", [P, T]), sb("linv", [P, T])
        score, rest, we = sb("score", [P, T, E]), sb("rest", [P, T, E]), sb("we", [P, T, E])
        top8 = sb("top8", [P, T, 8])
        weT = sb("weT", [E, B * L])
        fexp, live = score, rest
        den, dinv, scal = sb("den", [P, T, G]), sb("dinv", [P, T, G]), sb("scal", [P, T, G])
        soft = sb("soft", [P, T, E])
        stk = sb("stk", [P, T, 2, P], F16)
        sck = sb("sck", [P, T, 2 * G], F16)
        stkT = sb("stkT", [P, 2, B * L], F16)
        sckT = sb("sckT", [P, B * L], F16)
        warm, unused = sb("warm", [P, P], F16), sb("unused", [P, 2])
        silu, act32 = sb("silu", [P, 2, CH]), sb("act32", [P, 2, CH])
        a_hi = w_all[:, :].bitcast(F16).rearrange("p (c n) -> p c n", c=NJ)
        a_lo = sb("a_lo", [P, NJ, B * L], F16)

        bank = [ctx.enter_context(nc.psum_tensor(f"bank{i}", [P, 512], F32)) for i in range(8)]
        QK = (4, 5)
        ENERGY = (0, 2, 1, 3)
        XH1T = (1, 3, 1, 3)
        MIX = (0, 2, 1, 3)
        XH2T = (0, 2, 6, 7)
        ROUTE, ROUTE_T = 6, 7
        GATE, UP, SCAL = (0, 1), (2, 3), (4, 5)

        ld = {n: sem("ld_" + n) for n in ("ctx0", "ctx1", "wqk", "bqk", "gates", "cst", "ind", "x0", "x1", "mg", "inv",
                                           "gate0", "gate1", "up0", "up1", "down")}
        s_mv1, s_mv2, s_rstd2 = sem("mv1_ready"), sem("mv2_ready"), sem("rstd2_ready")
        s_stk0, s_warm = sem("stack_ends_cleared"), sem("warm_cleared")
        s_zero, s_id16, s_ind16 = sem("zeroed"), sem("id16_ready"), sem("ind16_ready")
        s_tg = sem("gates_tanh")
        s_q, s_k, s_qc, s_kc = sem("q_ready"), sem("k_ready"), sem("q_copied"), sem("k_copied")
        s_rstd1, s_rinv = sem("rstd1_ready"), sem("rinv_ready")
        s_xh1 = [sem(f"chunk{ch}_xh1_ready") for ch in range(NCH)]
        s_e, s_rmax, s_exp = sem("energy_ready"), sem("rowmax_ready"), sem("exp_ready")
        s_att = [sem(f"chunk{ch}_att_ready") for ch in range(NCH)]
        s_attT, s_attTc = sem("attT_ready"), sem("attT_copied")
        s_xhT, s_xhTc = sem("xh1T_ready"), sem("xh1T_copied")
        s_xm, s_x1, s_xh2 = sem("xm_ready"), sem("x1_ready"), sem("xh2_ready")
        s_x2T, s_x2hi, s_x2lo = sem("xh2T_ready"), sem("xT_hi_ready"), sem("xT_lo_ready")
        s_lg, s_lmax, s_lexp, s_we = sem("logits_ready"), sem("lmax_ready"), sem("lexp_ready"), sem("we_ready")
        s_weT, s_weTc = sem("weT_ready"), sem("weT_copied")
        s_fl, s_fexp, s_dinv = sem("flat_ready"), sem("fexp_ready"), sem("dinv_ready")
        s_stk, s_stT, s_stTc = sem("stack_ready"), sem("stackT_ready"), sem("stackT_copied")
        s_onehot = sem("onehot_ready")
        s_whi = [sem("gate_hi_ready"), sem("up_hi_ready")]
        s_wlo = [[sem(f"{name}{piece}_lo_ready") for piece in range(2)] for name in ("gate", "up")]
        s_dhi, s_dlo = sem("down_hi_ready"), sem("down_lo_ready")
        s_mghi, s_mglo, s_pad = sem("mask_gw_hi_ready"), sem("mask_gw_lo_ready"), sem("pad_ready")
        s_mup, s_muhi, s_mu = sem("mu_psum_ready"), sem("mu_hi_ready"), sem("mu_ready")
        s_g, s_u, s_sc = sem("g_ready"), sem("u_ready"), sem("sc_ready")
        s_silu, s_a, s_ahi, s_alo = sem("silu_ready"), sem("act_ready"), sem("a_hi_ready"), sem("a_lo_ready")
        s_prod, s_y0 = sem("silu_up_ready"), sem("y0_added")
        s_y, s_out, s_st = sem("y_ready"), sem("out_ready"), sem("stored")
        dve_step, pool_step = sem("dve_step"), sem("pool_step")

        SEG = mu_segments()
        DOWN_PIECES = [(n * NJ // 4, (n + 1) * NJ // 4) for n in range(4)]
        MU_BANK = (4, 5)
        WARM_UP = 34
        ident = cst[:, K_ID:K_ID + P]
        neg_mu = cst[:, K_NEG:K_NEG + 1]
        xv = x.rearrange("b (t p) d -> p (b t) d", p=P)
        ov = out.rearrange("b (t p) d -> p (b t) d", p=P)

        def pad_window(pad, k, s, slot):
            return pad[:, k, s, (P - GS) * slot:(P - GS) * slot + P]

        block = ctx.enter_context(nc.Block())

        @block.sync
        def _(sp):
            def weights(w, piece):
                name, src = (("gate", gateT), ("up", upT))[w]
                cols = (slice(0, EDGE), slice(EDGE, GI))[piece]
                sp.dma_start(w32[w][:, :, cols], src.rearrange("(k p) j -> p k j", p=P)[:, :, cols]
                             ).then_inc(ld[f"{name}{piece}"], 16)

            sp.dma_start(wqk_sb[:, :, :], wqkT.rearrange("p (w c) -> p w c", w=2)).then_inc(ld["wqk"], 16)
            sp.dma_start(x_sb[:, 0:TC, :], xv[:, 0:TC, :]).then_inc(ld["x0"], 16)
            sp.dma_start(gates_sb[:, :], gates.partition_broadcast(P)).then_inc(ld["gates"], 16)
            sp.dma_start(mg32[:, :, :], maskgwT.rearrange("(k p) e -> p k e", p=P)).then_inc(ld["mg"], 16)
            sp.dma_start(cst[:, :], consts).then_inc(ld["cst"], 16)
            weights(0, 0)
            sp.dma_start(ctx_sb[:, CH:], ctxT[:, CH:]).then_inc(ld["ctx1"], 16)
            sp.dma_start(inv_i[:, :], inv_map.partition_broadcast(E)).then_inc(ld["inv"], 16)
            weights(1, 0)
            sp.dma_start(x_sb[:, TC:T, :], xv[:, TC:T, :]).then_inc(ld["x1"], 16)
            weights(0, 1)
            weights(1, 1)
            sp.dma_start(ind32[:, :], ind).then_inc(ld["ind"], 16)
            sp.dma_start(down32[:, :, :], downT.rearrange("(c p) d -> p c d", p=P)).then_inc(ld["down"], 16)
            with sp.Fori(0, T) as t:
                sp.wait_ge(s_out, t + 1)
                sp.dma_start(ov[:, bass.ds(t, 1), :], x_sb[:, bass.ds(t, 1), :]).then_inc(s_st, 16)
            sp.wait_ge(s_st, 16 * T)

        @block.tensor
        def _(pe):
            def split_mm(dst, lhi, llo, rhi, rlo, start, stop):
                pe.matmul(dst, lhi, rhi, start=start, stop=False)
                pe.matmul(dst, lhi, rlo, start=False, stop=False)
                return pe.matmul(dst, llo, rhi, start=False, stop=stop)

            def project(ch):
                n = slice(ch * CH, (ch + 1) * CH)
                pe.matmul(bank[QK[1]][:, :], wqk_sb[:, 1, :], ctx_sb[:, n], start=True, stop=True).then_inc(s_k, 1)
                pe.matmul(bank[QK[0]][:, :], wqk_sb[:, 0, :], ctx_sb[:, n], start=True, stop=True).then_inc(s_q, 1)

            def energy(b):
                for t in range(TB):
                    m = b * L + t * P
                    i = pe.matmul(bank[ENERGY[b]][:, t * L:(t + 1) * L], qT[:, m:m + P], kT[:, b * L:(b + 1) * L],
                                  start=True, stop=True)
                i.then_inc(s_e, 1)

            def transpose_batch(b, src, dst_bank, done):
                for k in range(KD):
                    for t in range(TB):
                        i = pe.transpose(dst_bank[:, k * L + t * P:k * L + (t + 1) * P],
                                         src[:, b * TB + t, k * P:(k + 1) * P], ident)
                i.then_inc(done, 1)

            def xh1_transpose(b):
                pe.wait_ge(s_xh1[b // BC], TB * (b % BC + 1))
                transpose_batch(b, xh1, bank[XH1T[b]], s_xhT)

            def att_transpose(b):
                pe.wait_ge(s_att[b // BC], TB * (b % BC + 1))
                transpose_batch(b, att, bank[ENERGY[b]], s_attT)

            def mix(b):
                pe.wait_ge(s_attTc, b + 1)
                pe.wait_ge(s_xhTc, b + 1)
                for t in range(TB):
                    for k in range(KD):
                        i = pe.matmul(bank[MIX[b]][:, t * L:(t + 1) * L], xh1T[:, b % 2, k, t * P:(t + 1) * P],
                                      attT[:, b, k, :], start=(k == 0), stop=(k == KD - 1))
                i.then_inc(s_xm, 1)

            def xh2_transpose(b):
                pe.wait_ge(s_xh2, b + 1)
                transpose_batch(b, xh2, bank[XH2T[b]], s_x2T)

            def logits(ch):
                if ch == 0:
                    pe.wait_ge(s_mglo, 1)
                pe.wait_ge(s_x2lo, BC * (ch + 1))
                for t in range(TC):
                    m = slice(ch * CH + t * P, ch * CH + (t + 1) * P)
                    dst = bank[ROUTE][:, t * E:(t + 1) * E]
                    for k in range(KD):
                        pe.matmul(dst, xT_lo[:, k, m], gw_lo[:, k, :], start=(k == 0), stop=False)
                        i = split_mm(dst, xT_hi[:, k, m], xT_lo[:, k, m], gw_hi[:, k, :], gw_lo[:, k, :],
                                     False, k == KD - 1)
                i.then_inc(s_lg, 1)

            def we_transpose(ch):
                pe.wait_ge(s_we, ch + 1)
                for t in range(TC):
                    i = pe.transpose(bank[ROUTE_T][0:E, t * P:(t + 1) * P], we[:, ch * TC + t, :], ident)
                i.then_inc(s_weT, 1)

            def gather(ch):
                if ch == 0:
                    pe.wait_ge(s_onehot, 1)
                pe.wait_ge(s_weTc, ch + 1)
                for t in range(TC):
                    i = pe.matmul(bank[ROUTE][:, t * E:(t + 1) * E],
                                  weT[:, ch * CH + t * P:ch * CH + (t + 1) * P], onehot[:, :],
                                  start=True, stop=True)
                i.then_inc(s_fl, 1)

            def stack_transpose(ch):
                if ch == 0:
                    pe.wait_ge(s_id16, 1)
                pe.wait_ge(s_stk, ch + 1)
                dst, dst_sc = bank[ROUTE_T][:, :].bitcast(F16), bank[ROUTE][:, :].bitcast(F16)
                for t in range(TC):
                    for s in range(2):
                        pe.transpose(dst[:, s * CH + t * P:s * CH + (t + 1) * P], stk[:, ch * TC + t, s, :],
                                     id16[:, :])
                    i = pe.transpose(dst_sc[0:2 * G, t * P:(t + 1) * P], sck[:, ch * TC + t, :], id16[:, :])
                i.then_inc(s_stT, 1)

            def mu_segment(n):
                s, slot, a, z = SEG[n]
                if n == 0:
                    pe.wait_ge(s_pad, 2)
                    pe.wait_ge(s_qc, 2)
                    pe.wait_ge(s_kc, 2)
                if n in (0, SG):
                    for w in range(2):
                        pe.wait_ge(s_wlo[w][s], KD)
                if n >= 2:
                    pe.wait_ge(s_mu, n - 1)
                for w in range(2):
                    dst = bank[MU_BANK[n % 2]][:, w * INNER:w * INNER + z - a]
                    for k in range(KD):
                        i = split_mm(dst, pad_window(pad_hi, k, s, slot), pad_window(pad_lo, k, s, slot),
                                     w_hi[w][:, k, a:z], w_lo[w][:, k, a:z], k == 0, k == KD - 1)
                i.then_inc(s_mup, 1)

            def tile_x(ch, w, c, par, used):
                if used is not None:
                    pe.wait_ge((s_silu, s_a)[w], used)
                n, col = slice(ch * CH, (ch + 1) * CH), bass.ds(c * P, P)
                for k in range(KD):
                    split_mm(bank[(GATE, UP)[w][par]][:, :], w_hi[w][:, k, col], w_lo[w][:, k, col],
                             xT_hi[:, k, n], xT_lo[:, k, n], k == 0, False)

            def tile_soft(ch, w, c, s, par):
                n, col = slice(ch * CH, (ch + 1) * CH), bass.ds(c * P, P)
                pe.matmul(bank[(GATE, UP)[w][par]][:, :], mu[:, w, col], stkT[:, s, n],
                          start=False, stop=True).then_inc((s_g, s_u)[w], 1)

            def tile_scalar(ch, c, par):
                n, col = slice(ch * CH, (ch + 1) * CH), bass.ds(c * P, P)
                pe.matmul(bank[SCAL[par]][:, :], ind16[:, col], sckT[:, n], start=True, stop=True).then_inc(s_sc, 1)

            def unit(ch, c, s, par, used):
                for w in range(2):
                    tile_x(ch, w, c, par, used)
                    tile_soft(ch, w, c, s, par)
                tile_scalar(ch, c, par)

            pe.wait_ge(s_warm, 1)
            for _ in range(WARM_UP):
                pe.matmul(bank[7][:, 0:P], warm[:, :], warm[:, :], start=True, stop=True)
            pe.wait_ge(ld["wqk"], 16)
            pe.wait_ge(ld["ctx0"], 16)
            project(0)
            pe.wait_ge(s_kc, 1)
            pe.wait_ge(s_qc, 1)
            energy(0)
            energy(1)
            pe.wait_ge(ld["cst"], 16)
            xh1_transpose(0)
            att_transpose(0)
            xh1_transpose(1)
            att_transpose(1)
            mix(0)
            mix(1)
            pe.wait_ge(ld["ctx1"], 16)
            project(1)
            xh2_transpose(0)
            pe.wait_ge(s_kc, 2)
            pe.wait_ge(s_qc, 2)
            energy(2)
            xh2_transpose(1)
            energy(3)
            logits(0)
            pe.wait_ge(s_wlo[0][0], KD)
            tile_x(0, 0, 0, 0, None)
            pe.wait_ge(s_wlo[1][0], KD)
            tile_x(0, 1, 0, 0, None)
            mu_segment(0)
            mu_segment(1)
            we_transpose(0)
            pe.wait_ge(s_exp, 3 * TB)
            xh1_transpose(2)
            mu_segment(2)
            gather(0)
            pe.wait_ge(s_exp, 4 * TB)
            xh1_transpose(3)
            mu_segment(3)
            mu_segment(4)
            pe.wait_ge(s_xhTc, 3)
            att_transpose(2)
            pe.wait_ge(s_xhTc, 4)
            att_transpose(3)
            mu_segment(5)
            mix(2)
            mu_segment(6)
            mix(3)
            stack_transpose(0)
            mu_segment(7)
            mu_segment(8)
            pe.wait_ge(s_stTc, 1)
            tile_soft(0, 0, 0, 0, 0)
            tile_soft(0, 1, 0, 0, 0)
            pe.wait_ge(s_x1, 3)
            tile_x(0, 0, 1, 1, None)
            pe.wait_ge(s_ind16, 1)
            pe.wait_ge(s_stTc, 2)
            pe.wait_ge(s_mu, len(SEG))
            tile_scalar(0, 0, 0)
            tile_soft(0, 0, 1, 0, 1)
            pe.wait_ge(s_x1, 4)
            tile_x(0, 1, 1, 1, None)
            tile_soft(0, 1, 1, 0, 1)
            tile_scalar(0, 1, 1)

            for c in range(1, NJ):
                if c >= 2:
                    unit(0, c, int(c >= SPLIT), c % 2, c - 1)
                if c == 1:
                    xh2_transpose(2)
                    xh2_transpose(3)
                elif c == 2:
                    logits(1)
                elif c == 5:
                    we_transpose(1)
                elif c == 6:
                    gather(1)
                elif c == 9:
                    stack_transpose(1)
            pe.wait_ge(s_stTc, 4)
            for s, first, last in ((0, 0, SPLIT // 2), (1, SPLIT // 2, NJ // 2)):
                with pe.Fori(first, last) as i:
                    for h in range(2):
                        unit(1, 2 * i + h, s, (NJ + h) % 2, NJ + 2 * i + h - 1)
            unit(1, NJ - 1, 1, (2 * NJ - 1) % 2, 2 * NJ - 2)

            def down_tile(t, h, used):
                if used is not None:
                    pe.wait_ge(s_out, used)
                tok = bass.ds(t * P, P)
                for c in range(NJ):
                    y = split_mm(bank[6 + h][:, 0:D], a_hi[:, c, tok], a_lo[:, c, tok],
                                 down_hl[:, c, 0, :], down_hl[:, c, 1, :], c == 0, c == NJ - 1)
                y.then_inc(s_y, 1)

            pe.wait_ge(s_dhi, len(DOWN_PIECES))
            pe.wait_ge(s_dlo, len(DOWN_PIECES))
            pe.wait_ge(s_ahi, NJ)
            pe.wait_ge(s_alo, NJ)
            down_tile(0, 0, None)
            down_tile(1, 1, None)
            with pe.Fori(1, TC // 2) as i:
                for h in range(2):
                    down_tile(2 * i + h, h, 2 * i + h - 1)
            pe.wait_ge(s_ahi, NCH * NJ)
            pe.wait_ge(s_alo, NCH * NJ)
            with pe.Fori(TC // 2, T // 2) as i:
                for h in range(2):
                    down_tile(2 * i + h, h, 2 * i + h - 1)

        @block.scalar
        def _(act):
            act.dma_start(ctx_sb[:, 0:CH], ctxT[:, 0:CH]).then_inc(ld["ctx0"], 16)
            act.dma_start(bqk_sb[:, :], bqk).then_inc(ld["bqk"], 16)

            def q_copy(ch):
                act.wait_ge(s_q, ch + 1)
                act.activation(qT[:, ch * CH:(ch + 1) * CH], bank[QK[0]][:, :], ACT.Identity,
                               bias=bqk_sb[:, 0:1]).then_inc(s_qc, 1)

            def exps(b):
                act.wait_ge(s_rmax, b + 1)
                for t in range(b * TB, (b + 1) * TB):
                    act.activation(att[:, t, :], bank[ENERGY[b]][:, (t % TB) * L:(t % TB + 1) * L], ACT.Exp,
                                   bias=rmax[:, t:t + 1], accum_out=rsum[:, t:t + 1]).then_inc(s_exp, 1)

            def attT_copy(b):
                act.wait_ge(s_attT, b + 1)
                act.copy(attT[:, b, :, :].rearrange("p k m -> p (k m)"), bank[ENERGY[b]][:, :]).then_inc(s_attTc, 1)

            def xh1T_copy(b):
                act.wait_ge(s_xhT, b + 1)
                if b >= 2:
                    act.wait_ge(s_xm, b - 1)
                act.copy(xh1T[:, b % 2, :, :].rearrange("p k n -> p (k n)"), bank[XH1T[b]][:, :]
                         ).then_inc(s_xhTc, 1)

            def x2_hi(b):
                act.wait_ge(s_x2T, b + 1)
                act.copy(xT_hi[:, :, b * L:(b + 1) * L],
                         bank[XH2T[b]][:, :].rearrange("p (k n) -> p k n", k=KD)).then_inc(s_x2hi, 1)

            def logit_exps(ch):
                act.wait_ge(s_lmax, ch + 1)
                for t in range(TC):
                    n = ch * TC + t
                    act.activation(score[:, n, :], bank[ROUTE][:, t * E:(t + 1) * E], ACT.Exp,
                                   bias=lmax[:, n:n + 1], accum_out=lsum[:, n:n + 1]).then_inc(s_lexp, 1)

            def weT_copy(ch):
                act.wait_ge(s_weT, ch + 1)
                act.copy(weT[:, ch * CH:(ch + 1) * CH], bank[ROUTE_T][0:E, :]).then_inc(s_weTc, 1)

            def flat_exp(ch):
                act.wait_ge(s_fl, ch + 1)
                act.activation(fexp[:, ch * TC:(ch + 1) * TC, :].rearrange("p t e -> p (t e)"),
                               bank[ROUTE][:, 0:TC * E], ACT.Exp).then_inc(s_fexp, 1)

            def stack_copy(ch, between=None):
                act.wait_ge(s_stT, ch + 1)
                n = slice(ch * CH, (ch + 1) * CH)
                act.copy(stkT[:, :, n], bank[ROUTE_T][:, :].bitcast(F16).rearrange("p (s n) -> p s n", s=2)
                         ).then_inc(s_stTc, 1)
                if between is not None:
                    mu_high(between)
                if ch == 0:
                    act.wait_ge(s_zero, 1)
                act.copy(sckT[0:2 * G, n], bank[ROUTE][:, :].bitcast(F16)[0:2 * G, 0:CH]).then_inc(s_stTc, 1)

            def weight_hi(w, piece):
                act.wait_ge(ld[f"{('gate', 'up')[w]}{piece}"], 16)
                cols = (slice(0, EDGE), slice(EDGE, GI))[piece]
                act.copy(w_hi[w][:, :, cols], w32[w][:, :, cols]).then_inc(s_whi[w], 1)

            def down_hi(n):
                c = slice(*DOWN_PIECES[n])
                act.copy(down_hl[:, c, 0, :], down32[:, c, :]).then_inc(s_dhi, 1)

            def mu_high(n):
                s, slot, a, z = SEG[n]
                act.wait_ge(s_mup, n + 1)
                if n >= 2:
                    act.wait_ge(s_mu, n - 1)
                act.copy(mu_hi[:, n % 2, :, 0:z - a],
                         bank[MU_BANK[n % 2]][:, 0:2 * INNER].rearrange("p (w j) -> p w j", w=2)[:, :, 0:z - a]
                         ).then_inc(s_muhi, 1)

            def gate_silu(n, par, used):
                act.wait_ge(s_g, n + 1)
                if used is not None:
                    act.wait_ge(s_a, used)
                act.activation(silu[:, par, :], bank[GATE[par]][:, :], ACT.Silu).then_inc(s_silu, 1)

            def activation_high(n, c, par, tok):
                act.wait_ge(s_a, n + 1)
                act.copy(a_hi[:, c, tok], act32[:, par, :]).then_inc(s_ahi, 1)

            def activate(n, c, par, tok, used):
                gate_silu(n, par, used)
                activation_high(n, c, par, tok)

            act.wait_ge(s_warm, 1)
            act.activation(unused[:, :], warm[:, 0:2], ACT.Tanh)
            act.wait_ge(ld["bqk"], 16)
            q_copy(0)
            act.wait_ge(ld["gates"], 16)
            act.activation(tg[:, :], gates_sb[:, :], ACT.Tanh).then_inc(s_tg, 1)
            act.wait_ge(ld["mg"], 16)
            act.copy(mg_hi[:, :, :], mg32[:, :, :]).then_inc(s_mghi, 1)
            exps(0)
            exps(1)
            xh1T_copy(0)
            attT_copy(0)
            xh1T_copy(1)
            attT_copy(1)
            weight_hi(0, 0)
            weight_hi(1, 0)
            weight_hi(0, 1)
            q_copy(1)
            x2_hi(0)
            x2_hi(1)
            exps(2)
            weight_hi(1, 1)
            logit_exps(0)
            exps(3)
            act.wait_ge(ld["ind"], 16)
            act.wait_ge(s_zero, 2)
            act.copy(ind16[0:2 * G, :], ind32[:, :]).then_inc(s_ind16, 1)
            act.wait_ge(ld["cst"], 16)
            act.copy(id16[:, :], ident).then_inc(s_id16, 1)
            mu_high(0)
            mu_high(1)
            weT_copy(0)
            xh1T_copy(2)
            mu_high(2)
            flat_exp(0)
            xh1T_copy(3)
            mu_high(3)
            mu_high(4)
            attT_copy(2)
            attT_copy(3)
            mu_high(5)
            mu_high(6)
            stack_copy(0, between=7)
            mu_high(8)
            for c in range(NJ):
                gate_silu(c, c % 2, c - 1 if c >= 2 else None)
                if c == 1:
                    x2_hi(2)
                    x2_hi(3)
                elif c == 3:
                    logit_exps(1)
                elif c == 5:
                    weT_copy(1)
                elif c == 7:
                    flat_exp(1)
                elif c == 10:
                    stack_copy(1)
                activation_high(c, c, c % 2, slice(0, CH))
                if c % 2 == 0 and c // 2 < len(DOWN_PIECES):
                    if c == 0:
                        act.wait_ge(ld["down"], 16)
                    down_hi(c // 2)
            tok1 = slice(CH, 2 * CH)
            with act.Fori(0, NJ // 2) as i:
                for h in range(2):
                    n = 2 * i + (NJ + h)
                    activate(n, bass.ds(2 * i + h, 1), (NJ + h) % 2, tok1, n - 1)
            activate(2 * NJ - 1, NJ - 1, (2 * NJ - 1) % 2, tok1, 2 * NJ - 2)

        @block.gpsimd
        def _(pool):
            def clear(tile):
                return pool.memset(tile.bitcast(F32) if tile.dtype == F16 else tile, 0.0)

            def reciprocal_root(var, rstd, src, b, batches, ready, done):
                r = slice(b * TB, (b + batches) * TB)
                pool.wait_ge(ready, b + batches)
                step(pool.tensor_scalar(var[:, r], src[:, r, 1], EPS, None, ALU.add))
                pool.tensor_tensor(rstd[:, r], var[:, r], half[:, 0:batches * TB], ALU.pow).then_inc(done, batches)

            steps = [0]

            def step(instruction):
                steps[0] += 1
                instruction.then_inc(pool_step, 1)
                pool.wait_ge(pool_step, steps[0])

            def weight_lo(w, piece, k):
                pool.wait_ge(s_whi[w], piece + 1)
                cols = (slice(0, EDGE), slice(EDGE, GI))[piece]
                pool.tensor_tensor(w_lo[w][:, k, cols], w32[w][:, k, cols], w_hi[w][:, k, cols],
                                   ALU.subtract).then_inc(s_wlo[w][piece], 1)

            def scale_att(b):
                pool.wait_ge(s_rinv, b + 1)
                for t in range(b * TB, (b + 1) * TB):
                    pool.tensor_scalar(att[:, t, :], att[:, t, :], rinv[:, t:t + 1], tg[:, 0:1],
                                       ALU.mult, ALU.mult).then_inc(s_att[b // BC], 1)

            def activation_low(n, c, par, tok):
                pool.wait_ge(s_ahi, n + 1)
                pool.tensor_tensor(a_lo[:, c, tok], act32[:, par, :], a_hi[:, c, tok],
                                   ALU.subtract).then_inc(s_alo, 1)

            step(pool.memset(half[:, :], -0.5))
            clear(pad_hi[:, :, :, :].rearrange("p k s w -> p (k s w)"))
            step(clear(pad_lo[:, :, :, :].rearrange("p k s w -> p (k s w)")))
            pool.memset(stk[:, :, :, 3 * COPY:], 0.0).then_inc(s_stk0, 1)
            clear(sckT[:, :]).then_inc(s_zero, 1)
            clear(ind16[:, :]).then_inc(s_zero, 1)
            reciprocal_root(var1, rstd1, mv, 0, 1, s_mv1, s_rstd1)
            reciprocal_root(var1, rstd1, mv, 1, 1, s_mv1, s_rstd1)
            pool.wait_ge(s_mghi, 1)
            pool.tensor_tensor(mg_lo[:, :, :], mg32[:, :, :], mg_hi[:, :, :], ALU.subtract).then_inc(s_mglo, 1)
            pool.wait_ge(s_mglo, 1)
            for pad, mask in ((pad_hi, mask_hi), (pad_lo, mask_lo)):
                for s, first in ((0, 0), (1, 1)):
                    for k in range(KD):
                        g0 = BASE[s] + first
                        dst = pad[:, k, s, :].rearrange("p (g w) -> p g w", w=P)[:, first:SG, 0:3 * COPY]
                        dst = dst.rearrange("p g (r c) -> p g r c", r=3)[:, :, :, 0:GS]
                        src = mask[:, k, g0 * GS:(g0 + SG - first) * GS].rearrange("p (g a i) -> p g a i", a=1, i=GS)
                        i = pool.tensor_copy(dst, src.to_broadcast([P, SG - first, 3, GS]))
                i.then_inc(s_pad, 1)
            pool.wait_ge(ld["inv"], 16)
            step(pool.tensor_copy(inv_f[:, :], inv_i[:, :]))
            step(pool.tensor_scalar(inv_n[:, :], inv_f[:, :], 0.0, float(E), ALU.is_lt, ALU.mult))
            step(pool.tensor_tensor(inv_f[:, :], inv_f[:, :], inv_n[:, :], ALU.add))
            step(pool.tensor_scalar(inv_f[:, :], inv_f[:, :], 0.0, float(E - 1), ALU.max, ALU.min))
            pool.wait_ge(ld["cst"], 16)
            pool.tensor_scalar(onehot[:, :], inv_f[:, :], cst[0:E, K_IOTA:K_IOTA + 1], None,
                               ALU.is_equal).then_inc(s_onehot, 1)
            weight_lo(0, 0, 0)
            reciprocal_root(var2, rstd2, mv2, 0, 1, s_mv2, s_rstd2)
            reciprocal_root(var2, rstd2, mv2, 1, 1, s_mv2, s_rstd2)
            weight_lo(0, 0, 1)
            reciprocal_root(var1, rstd1, mv, 2, 2, s_mv1, s_rstd1)
            weight_lo(0, 1, 0)
            weight_lo(0, 1, 1)
            weight_lo(1, 1, 0)
            weight_lo(1, 1, 1)
            scale_att(2)
            scale_att(3)
            for c in range(NJ):
                if c == 0:
                    reciprocal_root(var2, rstd2, mv2, 2, 2, s_mv2, s_rstd2)
                activation_low(c, c, c % 2, slice(0, CH))
                if c % 2 and c // 2 < len(DOWN_PIECES):
                    n = c // 2
                    pool.wait_ge(s_dhi, n + 1)
                    d = slice(*DOWN_PIECES[n])
                    pool.tensor_tensor(down_hl[:, d, 1, :], down32[:, d, :], down_hl[:, d, 0, :],
                                       ALU.subtract).then_inc(s_dlo, 1)
            tok1 = slice(CH, 2 * CH)
            with pool.Fori(0, NJ // 2) as i:
                for h in range(2):
                    activation_low(2 * i + (NJ + h), bass.ds(2 * i + h, 1), (NJ + h) % 2, tok1)
            activation_low(2 * NJ - 1, NJ - 1, (2 * NJ - 1) % 2, tok1)

        @block.vector
        def _(dve):
            steps = [0]

            def step(instruction):
                steps[0] += 1
                instruction.then_inc(dve_step, 1)
                dve.wait_ge(dve_step, steps[0])

            def statistics(mean_var, stat, b, done):
                tiles = range(b * TB, (b + 1) * TB)
                for t in tiles:
                    i = dve.bn_stats(stat[:, t % TC, :], x_sb[:, t, :])
                step(i)
                for t in tiles:
                    i = dve.bn_aggr(mean_var[:, t, :], stat[:, t % TC, :])
                i.then_inc(done, 1)

            def statistics1(b):
                dve.wait_ge(ld[f"x{b // BC}"], 16)
                statistics(mv, stats, b, s_mv1)

            def normalise1(b):
                dve.wait_ge(s_rstd1, b + 1)
                for t in range(b * TB, (b + 1) * TB):
                    dve.tensor_scalar(xh1[:, t, :], x_sb[:, t, :], mv[:, t, 0:1], rstd1[:, t:t + 1],
                                      ALU.subtract, ALU.mult).then_inc(s_xh1[b // BC], 1)

            def k_copy(ch):
                dve.wait_ge(s_k, ch + 1)
                dve.tensor_scalar(kT[:, ch * CH:(ch + 1) * CH], bank[QK[1]][:, :], bqk_sb[:, 1:2], None,
                                  ALU.add).then_inc(s_kc, 1)

            def row_max(b):
                dve.wait_ge(s_e, b + 1)
                dve.tensor_reduce(rmax[:, b * TB:(b + 1) * TB],
                                  bank[ENERGY[b]][:, :].rearrange("p (t n) -> p t n", t=TB), AX.X, ALU.max,
                                  negate=True).then_inc(s_rmax, 1)

            def sum_reciprocal(b):
                dve.wait_ge(s_exp, (b + 1) * TB)
                dve.reciprocal(rinv[:, b * TB:(b + 1) * TB], rsum[:, b * TB:(b + 1) * TB]).then_inc(s_rinv, 1)

            def scale_att(b):
                sum_reciprocal(b)
                dve.wait_ge(s_rinv, b + 1)
                for t in range(b * TB, (b + 1) * TB):
                    dve.tensor_scalar(att[:, t, :], att[:, t, :], rinv[:, t:t + 1], tg[:, 0:1],
                                      ALU.mult, ALU.mult).then_inc(s_att[b // BC], 1)

            def residual(b):
                r = slice(b * TB, (b + 1) * TB)
                dve.wait_ge(s_xm, b + 1)
                dve.tensor_tensor(x_sb[:, r, :].rearrange("p t d -> p (t d)"), bank[MIX[b]][:, :],
                                  x_sb[:, r, :].rearrange("p t d -> p (t d)"), ALU.add).then_inc(s_x1, 1)

            def statistics2(b):
                dve.wait_ge(s_x1, b + 1)
                statistics(mv2, stats2, b, s_mv2)

            def normalise2(b):
                dve.wait_ge(s_rstd2, b + 1)
                for t in range(b * TB, (b + 1) * TB):
                    i = dve.tensor_scalar(xh2[:, t, :], x_sb[:, t, :], mv2[:, t, 0:1], rstd2[:, t:t + 1],
                                          ALU.subtract, ALU.mult)
                i.then_inc(s_xh2, 1)

            def x2_lo(b):
                dve.wait_ge(s_x2hi, b + 1)
                dve.tensor_tensor(xT_lo[:, :, b * L:(b + 1) * L],
                                  bank[XH2T[b]][:, :].rearrange("p (k n) -> p k n", k=KD),
                                  xT_hi[:, :, b * L:(b + 1) * L], ALU.subtract).then_inc(s_x2lo, 1)

            def logit_max(ch):
                dve.wait_ge(s_lg, ch + 1)
                dve.tensor_reduce(lmax[:, ch * TC:(ch + 1) * TC],
                                  bank[ROUTE][:, 0:TC * E].rearrange("p (t e) -> p t e", t=TC), AX.X, ALU.max,
                                  negate=True).then_inc(s_lmax, 1)

            def top_scores(ch):
                r, tiles = slice(ch * TC, (ch + 1) * TC), range(ch * TC, (ch + 1) * TC)
                dve.wait_ge(s_lexp, (ch + 1) * TC)
                step(dve.reciprocal(linv[:, r], lsum[:, r]))
                for t in tiles:
                    i = dve.tensor_scalar(score[:, t, :], score[:, t, :], linv[:, t:t + 1], None, ALU.mult)
                step(i)
                for t in tiles:
                    i = dve.max(top8[:, t, :], score[:, t, :])
                step(i)
                for t in tiles:
                    i = dve.match_replace(rest[:, t, :], top8[:, t, :], score[:, t, :], 0.0)
                step(i)
                dve.tensor_tensor(we[:, r, :], score[:, r, :], rest[:, r, :], ALU.subtract).then_inc(s_we, 1)

            def grouped(tile, r):
                return tile[:, r, :].rearrange("p t (g i) -> p (t g) i", i=GS)

            def slot_softmax(ch):
                r = slice(ch * TC, (ch + 1) * TC)
                flat = bank[ROUTE][:, 0:TC * E]

                def flattened(tile):
                    return tile[:, r, :].rearrange("p t e -> p (t e)")

                dve.wait_ge(s_fexp, ch + 1)
                step(dve.tensor_scalar(flattened(live), flat, 0.0, TINY, ALU.not_equal, ALU.max))
                dve.tensor_reduce(flattened(scal), flat.rearrange("p (g i) -> p g i", i=GS), AX.X, ALU.add)
                step(dve.tensor_tensor(fexp[:, r, :], fexp[:, r, :], live[:, r, :], ALU.mult))
                step(dve.tensor_reduce(flattened(den), grouped(fexp, r), AX.X, ALU.add))
                dve.reciprocal(dinv[:, r, :], den[:, r, :]).then_inc(s_dinv, 1)

            def make_stacks(ch):
                r = slice(ch * TC, (ch + 1) * TC)
                dve.wait_ge(s_dinv, ch + 1)
                step(dve.tensor_tensor(grouped(soft, r), grouped(fexp, r),
                                       dinv[:, r, :].rearrange("p t (g a) -> p (t g) a", a=1)
                                       .to_broadcast([P, TC * G, GS]), ALU.mult))
                if ch == 0:
                    dve.wait_ge(s_stk0, 1)
                dve.tensor_scalar(sck[:, r, 0:G], scal[:, r, :], SC_SCALE, None, ALU.mult)
                for s in range(2):
                    src = soft[:, r, BASE[s] * GS:BASE[s] * GS + COPY]
                    dve.tensor_copy(stk[:, r, s, 0:COPY], src)
                    i = dve.tensor_copy(stk[:, r, s, COPY:2 * COPY], src)
                step(i)
                for s in range(2):
                    src = soft[:, r, BASE[s] * GS:BASE[s] * GS + COPY]
                    dve.tensor_tensor(stk[:, r, s, 2 * COPY:3 * COPY], src, stk[:, r, s, 0:COPY], ALU.subtract)
                dve.scalar_tensor_tensor(sck[:, r, G:2 * G], scal[:, r, :], SC_SCALE, sck[:, r, 0:G],
                                         ALU.mult, ALU.subtract).then_inc(s_stk, 1)

            def weight_lo(w, piece, k):
                dve.wait_ge(s_whi[w], piece + 1)
                cols = (slice(0, EDGE), slice(EDGE, GI))[piece]
                dve.tensor_tensor(w_lo[w][:, k, cols], w32[w][:, k, cols], w_hi[w][:, k, cols],
                                  ALU.subtract).then_inc(s_wlo[w][piece], 1)

            def mu_stack(n):
                s, slot, a, z = SEG[n]
                dve.wait_ge(s_muhi, n + 1)
                dve.scalar_tensor_tensor(mu[:, :, a:z], mu_hi[:, n % 2, :, 0:z - a], neg_mu,
                                         bank[MU_BANK[n % 2]][:, 0:2 * INNER]
                                         .rearrange("p (w j) -> p w j", w=2)[:, :, 0:z - a],
                                         ALU.mult, ALU.add).then_inc(s_mu, 1)

            def multiply(n, par, low):
                dve.wait_ge(s_silu, n + 1)
                dve.wait_ge(s_u, n + 1)
                dve.tensor_tensor(silu[:, par, :], silu[:, par, :], bank[UP[par]][:, :], ALU.mult
                                  ).then_inc(s_prod, 1)
                dve.wait_ge(s_prod, n + 1)
                dve.wait_ge(s_sc, n + 1)
                if low is not None:
                    dve.wait_ge(s_ahi, low)
                    dve.wait_ge(s_alo, low)
                dve.tensor_tensor(act32[:, par, :], silu[:, par, :], bank[SCAL[par]][:, :], ALU.mult
                                  ).then_inc(s_a, 1)

            dve.memset(warm[:, :].bitcast(F32), 0.0).then_inc(s_warm, 1)
            statistics1(0)
            dve.wait_ge(ld["bqk"], 16)
            k_copy(0)
            statistics1(1)
            row_max(0)
            normalise1(0)
            row_max(1)
            dve.wait_ge(s_tg, 1)
            scale_att(0)
            normalise1(1)
            scale_att(1)
            statistics1(2)
            statistics1(3)
            residual(0)
            statistics2(0)
            residual(1)
            statistics2(1)
            normalise2(0)
            k_copy(1)
            normalise2(1)
            x2_lo(0)
            row_max(2)
            x2_lo(1)
            weight_lo(1, 0, 0)
            weight_lo(1, 0, 1)
            logit_max(0)
            row_max(3)
            normalise1(2)
            sum_reciprocal(2)
            top_scores(0)
            sum_reciprocal(3)
            normalise1(3)
            for n in range(5):
                mu_stack(n)
            slot_softmax(0)
            mu_stack(5)
            make_stacks(0)
            residual(2)
            mu_stack(6)
            residual(3)
            statistics2(2)
            mu_stack(7)
            statistics2(3)
            mu_stack(8)
            for c in range(NJ):
                multiply(c, c % 2, c - 1 if c >= 2 else None)
                if c in (0, 1):
                    for b in (2, 3):
                        (normalise2, x2_lo)[c](b)
                elif c == 2:
                    logit_max(1)
                elif c == 3:
                    top_scores(1)
                elif c == 7:
                    slot_softmax(1)
                elif c == 8:
                    make_stacks(1)
            with dve.Fori(0, NJ // 2) as i:
                for h in range(2):
                    n = 2 * i + (NJ + h)
                    multiply(n, (NJ + h) % 2, n - 1)
            multiply(2 * NJ - 1, (2 * NJ - 1) % 2, 2 * NJ - 2)

            with dve.Fori(0, T // 2) as i:
                for h in range(2):
                    t = 2 * i + h
                    row = x_sb[:, bass.ds(t, 1), :].rearrange("p t d -> p (t d)")
                    dve.wait_ge(s_y, t + 1)
                    dve.scalar_tensor_tensor(row, bank[6 + h][:, 0:D], tg[:, 1:2], row,
                                             ALU.mult, ALU.add).then_inc(s_out, 1)


_OUT = ((B, L, D), "float32")


def kernel(x, ctx_1024, g_xattn, g_ffn, L0_xattn_Wq, L0_xattn_bq, L0_xattn_Wk, L0_xattn_bk, L0_ffn_gate_w,
           L0_ffn_mask_up_w, L0_ffn_gate_proj_w, L0_ffn_up_proj_w, L0_ffn_down_proj_w, L0_ffn_inv_map):
    import concourse.bacc as bacc
    from concourse.bass_utils import run_bass_kernel_spmd

    inv = np.ascontiguousarray(L0_ffn_inv_map).reshape(-1)
    if inv.dtype.itemsize == 8:
        inv = inv.view(np.int32)[::2]
    arrays = {
        "ctxT": np.asarray(ctx_1024).reshape(B * L, C).T,
        "x": np.asarray(x),
        "wqkT": np.concatenate([np.asarray(L0_xattn_Wq).T, np.asarray(L0_xattn_Wk).T], 1),
        "bqk": np.stack([np.asarray(L0_xattn_bq), np.asarray(L0_xattn_bk)], 1),
        "gates": np.concatenate([np.asarray(g_xattn), np.asarray(g_ffn)]),
        "gateT": np.asarray(L0_ffn_gate_proj_w).reshape(GI, D).T,
        "upT": np.asarray(L0_ffn_up_proj_w).reshape(GI, D).T,
        "downT": np.asarray(L0_ffn_down_proj_w).transpose(0, 2, 1).reshape(GI, D),
        "maskgwT": np.concatenate([np.asarray(L0_ffn_mask_up_w).transpose(1, 0, 2).reshape(D, E),
                                   np.asarray(L0_ffn_gate_w).T], 1),
        "inv_map": inv,
        "consts": constants(),
        "ind": indicator(),
    }
    arrays = {f"in_{k}": np.ascontiguousarray(v) for k, v in arrays.items()}
    nc = bacc.Bacc("TRN2", target_bir_lowering=False, num_devices=1)
    args = [nc.dram_tensor(k, v.shape, mybir.dt.from_np(v.dtype), kind="ExternalInput").ap()
            for k, v in arrays.items()]
    out = nc.dram_tensor("out", _OUT[0], mybir.dt.from_np(np.dtype(_OUT[1])), kind="ExternalOutput").ap()
    block_kernel(nc, *args, out)
    r = run_bass_kernel_spmd(nc, [arrays], core_ids=[0])
    return r.results[0]["out"]
```

```python
from contextlib import ExitStack

import numpy as np

import concourse.bass as bass
from concourse import mybir

ALU = mybir.AluOpType
ACT = mybir.ActivationFunctionType
AX = mybir.AxisListType
F32 = mybir.dt.float32
F16 = mybir.dt.float16
I32 = mybir.dt.int32

P = 128
B, L, D = 4, 256, 256
C = 128
E, G, GS, INNER = 64, 8, 8, 176
T = B * L // P
TB = L // P
KD = D // P
CH = 512
NCH = B * L // CH
TC = CH // P
BC = CH // L
GI = G * INNER
NJ = GI // P
SG = 5
COPY = SG * GS
BASE = (0, G - SG)
SPLIT = 6
EPS = 1e-5
TINY = 2.0 ** -40
EDGE = SPLIT * P


def mu_blocks():
    pieces = ([], [])
    for g in range(G):
        a, z = g * INNER, (g + 1) * INNER
        if a < EDGE:
            pieces[0].append((g - BASE[0], a, min(z, EDGE)))
        if z > EDGE:
            pieces[1].append((g - BASE[1], max(a, EDGE), z))
    first, second = ((p[:len(p) // 2], p[len(p) // 2:]) for p in pieces)
    return [(0, 0, first[0]), (0, 0, first[1]), (1, 0, first[0]), (1, 0, first[1]),
            (0, 1, second[0]), (1, 1, second[0]), (0, 1, second[1]), (1, 1, second[1])]


K_ID, K_NEG, K_IOTA, K_END = 0, P, P + 1, P + 2


def constants():
    c = np.zeros((P, K_END), np.float32)
    c[:, K_ID:K_ID + P] = np.eye(P)
    c[COPY:2 * COPY, K_NEG] = -1.0
    c[:, K_IOTA] = np.arange(P)
    return c


def scalar_pieces(c):
    first, edge = c * P // INNER, (c * P // INNER + 1) * INNER - c * P
    if edge < P:
        return (first, 0, edge), (first + 1, edge, P)
    return (first, 0, P // 2), (first, P // 2, P)


def block_kernel(nc, ctxT, x, xT, wqkT, bqk, gates, gateT, upT, downT, maskgwT, inv_map, consts, out):
    with ExitStack() as ctx:
        def sb(name, shape, dt=F32):
            return ctx.enter_context(nc.sbuf_tensor(name, shape, dt))

        def sem(name):
            return ctx.enter_context(nc.semaphore(name))

        ctx_sb = sb("ctx_sb", [P, B * L])
        wqk_sb, bqk_sb = sb("wqk_sb", [P, 2, C]), sb("bqk_sb", [P, 2])
        gates_sb, tg = sb("gates_sb", [P, 2]), sb("tg", [P, 2])
        cst = sb("cst", [P, K_END])
        x_sb = sb("x_sb", [P, T, D])
        w_all = sb("w_all", [P, 2 * KD * GI])
        w32 = [w_all[:, w * KD * GI:(w + 1) * KD * GI].rearrange("p (k j) -> p k j", k=KD) for w in range(2)]
        w_hi = [sb("gate_hi", [P, KD, GI], F16), sb("up_hi", [P, KD, GI], F16)]
        w_lo = [sb("gate_lo", [P, KD, GI], F16), sb("up_lo", [P, KD, GI], F16)]
        down32 = sb("down32", [P, NJ, D])
        down_hl = sb("down_hl", [P, NJ, 2, D], F16)
        mg32 = sb("mg32", [P, KD, 2 * E])
        mg_hi, mg_lo = sb("mg_hi", [P, KD, 2 * E], F16), sb("mg_lo", [P, KD, 2 * E], F16)
        mask_hi, mask_lo, gw_hi, gw_lo = mg_hi[:, :, 0:E], mg_lo[:, :, 0:E], mg_hi[:, :, E:], mg_lo[:, :, E:]
        pad_hi = sb("pad_hi", [P, KD, 2, SG * P], F16)
        pad_lo = sb("pad_lo", [P, KD, 2, SG * P], F16)
        mu = sb("mu", [P, 2, GI], F16)
        inv_i, inv_f, inv_n = sb("inv_i", [E, E], I32), sb("inv_f", [E, E]), sb("inv_n", [E, E])
        onehot = sb("onehot", [E, E])
        id16 = sb("id16", [P, P], F16)
        qT, kT = sb("qT", [P, B * L]), sb("kT", [P, B * L])
        stats, mv = sb("stats", [P, TC, 6]), sb("mv", [P, T, 2])
        stats2, mv2 = sb("stats2", [P, TC, 6]), sb("mv2", [P, T, 2])
        half = sb("half", [P, TC])
        var1, rstd1 = sb("var1", [P, T]), sb("rstd1", [P, T])
        mr1, shift1 = sb("mr1", [P, T]), sb("shift1", [P, T])
        var2, rstd2 = sb("var2", [P, T]), sb("rstd2", [P, T])
        rmax, rsum, rinv = sb("rmax", [P, T]), sb("rsum", [P, T]), sb("rinv", [P, T])
        att = sb("att", [P, T, L])
        xT_sb, attT = sb("xT_sb", [P, KD, B * L]), sb("attT", [P, B, TB, L])
        xh2 = att
        xT_hi, xT_lo = sb("xT_hi", [P, KD, B * L], F16), sb("xT_lo", [P, KD, B * L], F16)
        lmax, lsum, linv = sb("lmax", [P, T]), sb("lsum", [P, T]), sb("linv", [P, T])
        score, rest, we = sb("score", [P, T, E]), sb("rest", [P, T, E]), sb("we", [P, T, E])
        top8 = sb("top8", [P, T, 8])
        weT = sb("weT", [E, B * L])
        fexp, live = score, rest
        den, dinv, scal = sb("den", [P, T, G]), sb("dinv", [P, T, G]), sb("scal", [P, T, G])
        soft = sb("soft", [P, T, E])
        stk = sb("stk", [P, T, 2, P], F16)
        stkT = sb("stkT", [P, 2, B * L], F16)
        scalT = sb("scalT", [G, B * L])
        scal_rows = sb("scal_rows", [P, 2, CH])
        warm, unused = sb("warm", [P, P], F16), sb("unused", [P, 2])
        silu, act32 = sb("silu", [P, 2, CH]), sb("act32", [P, 2, CH])
        a_hi = w_all[:, :].bitcast(F16).rearrange("p (c n) -> p c n", c=NJ)
        a_lo = sb("a_lo", [P, NJ, B * L], F16)

        bank = [ctx.enter_context(nc.psum_tensor(f"bank{i}", [P, 512], F32)) for i in range(8)]
        QK = ((4, 5), (6, 7))
        ENERGY = (0, 2, 1, 3)
        MIX = (0, 2, 1, 3)
        XH2T = (0, 2, 6, 7)
        ROUTE, ROUTE_T = 6, 7
        GATE, UP = (0, 1), (2, 3)

        ld = {n: sem("ld_" + n) for n in ("ctx0", "ctx1", "wqk", "bqk", "gates", "cst", "x0", "x1", "xT0", "xT1", "mg", "inv",
                                           "gate0", "gate1", "up0", "up1", "down")}
        s_mv1, s_mv2, s_rstd2 = sem("mv1_ready"), sem("mv2_ready"), sem("rstd2_ready")
        s_stk0, s_warm = sem("stack_ends_cleared"), sem("warm_cleared")
        s_id16 = sem("id16_ready")
        s_sc, s_scT, s_scTc = sem("scalars_ready"), sem("scalarsT_ready"), sem("scalarsT_copied")
        s_rows = [sem(f"scalar_rows{par}") for par in range(2)]
        s_tg = sem("gates_tanh")
        s_q, s_k, s_qc, s_kc = sem("q_ready"), sem("k_ready"), sem("q_copied"), sem("k_copied")
        s_rstd1, s_rinv = sem("rstd1_ready"), sem("rinv_ready")
        s_shift, s_xc = sem("shift1_ready"), sem("x_shifted")
        s_e, s_rmax, s_exp = sem("energy_ready"), sem("rowmax_ready"), sem("exp_ready")
        s_att = [sem(f"chunk{ch}_att_ready") for ch in range(NCH)]
        s_attT, s_attTc = sem("attT_ready"), sem("attT_copied")
        s_xm, s_x1, s_xh2 = sem("xm_ready"), sem("x1_ready"), sem("xh2_ready")
        s_x2T, s_x2hi, s_x2lo = sem("xh2T_ready"), sem("xT_hi_ready"), sem("xT_lo_ready")
        s_lg, s_lmax, s_lexp, s_we = sem("logits_ready"), sem("lmax_ready"), sem("lexp_ready"), sem("we_ready")
        s_weT, s_weTc = sem("weT_ready"), sem("weT_copied")
        s_fl, s_fexp, s_dinv = sem("flat_ready"), sem("fexp_ready"), sem("dinv_ready")
        s_stk, s_stT, s_stTc = sem("stack_ready"), sem("stackT_ready"), sem("stackT_copied")
        s_onehot = sem("onehot_ready")
        s_whi = [sem("gate_hi_ready"), sem("up_hi_ready")]
        s_wlo = [[sem(f"{name}{piece}_lo_ready") for piece in range(2)] for name in ("gate", "up")]
        s_dhi, s_dlo = sem("down_hi_ready"), sem("down_lo_ready")
        s_mghi, s_mglo, s_pad = sem("mask_gw_hi_ready"), sem("mask_gw_lo_ready"), sem("pad_ready")
        s_mup, s_muhi, s_mu = sem("mu_psum_ready"), sem("mu_hi_ready"), sem("mu_ready")
        s_g, s_u = sem("g_ready"), sem("u_ready")
        s_silu, s_a, s_ahi, s_alo = sem("silu_ready"), sem("act_ready"), sem("a_hi_ready"), sem("a_lo_ready")
        s_prod, s_y0 = sem("silu_up_ready"), sem("y0_added")
        s_y, s_out, s_st = sem("y_ready"), sem("out_ready"), sem("stored")
        dve_step, pool_step = sem("dve_step"), sem("pool_step")

        MU = mu_blocks()
        MU_COLS = max(b[2][-1][2] - b[2][0][1] for b in MU)
        DOWN_PIECES = [(n * NJ // 4, (n + 1) * NJ // 4) for n in range(4)]
        MU_BANK = (4, 5)
        mu_hi = sb("mu_hi", [P, 2, MU_COLS], F16)
        WARM_UP = 34
        ident = cst[:, K_ID:K_ID + P]
        neg_mu = cst[:, K_NEG:K_NEG + 1]
        xv = x.rearrange("b (t p) d -> p (b t) d", p=P)
        ov = out.rearrange("b (t p) d -> p (b t) d", p=P)

        def pad_window(pad, k, s, slot):
            return pad[:, k, s, (P - GS) * slot:(P - GS) * slot + P]

        block = ctx.enter_context(nc.Block())

        @block.sync
        def _(sp):
            def weights(w, piece):
                name, src = (("gate", gateT), ("up", upT))[w]
                cols = (slice(0, EDGE), slice(EDGE, GI))[piece]
                sp.dma_start(w32[w][:, :, cols], src.rearrange("(k p) j -> p k j", p=P)[:, :, cols]
                             ).then_inc(ld[f"{name}{piece}"], 16)

            xTv = xT.rearrange("(k p) n -> p k n", p=P)
            sp.dma_start(wqk_sb[:, :, :], wqkT.rearrange("p (w c) -> p w c", w=2)).then_inc(ld["wqk"], 16)
            sp.dma_start(gates_sb[:, :], gates.partition_broadcast(P)).then_inc(ld["gates"], 16)
            sp.dma_start(mg32[:, :, :], maskgwT.rearrange("(k p) e -> p k e", p=P)).then_inc(ld["mg"], 16)
            sp.dma_start(x_sb[:, 0:TC, :], xv[:, 0:TC, :]).then_inc(ld["x0"], 16)
            weights(0, 0)
            sp.dma_start(ctx_sb[:, CH:], ctxT[:, CH:]).then_inc(ld["ctx1"], 16)
            sp.dma_start(cst[:, :], consts).then_inc(ld["cst"], 16)
            sp.dma_start(xT_sb[:, :, 0:CH], xTv[:, :, 0:CH]).then_inc(ld["xT0"], 16)
            sp.dma_start(inv_i[:, :], inv_map.partition_broadcast(E)).then_inc(ld["inv"], 16)
            weights(1, 0)
            sp.dma_start(x_sb[:, TC:T, :], xv[:, TC:T, :]).then_inc(ld["x1"], 16)
            weights(0, 1)
            weights(1, 1)
            sp.dma_start(xT_sb[:, :, CH:], xTv[:, :, CH:]).then_inc(ld["xT1"], 16)
            sp.dma_start(down32[:, :, :], downT.rearrange("(c p) d -> p c d", p=P)).then_inc(ld["down"], 16)
            for n in range(NCH * NJ):
                ch, c = n // NJ, n % NJ
                if c == 0:
                    sp.wait_ge(s_scTc, ch + 1)
                if n >= 2:
                    sp.wait_ge(s_prod, n - 1)
                for g, a, z in scalar_pieces(c):
                    row = scalT[g:g + 1, ch * CH:(ch + 1) * CH].rearrange("g (a n) -> g a n", a=1)
                    sp.dma_start(scal_rows[a:z, n % 2, :],
                                 row.to_broadcast([1, z - a, CH])).then_inc(s_rows[n % 2], 16)
            with sp.Fori(0, T) as t:
                sp.wait_ge(s_out, t + 1)
                sp.dma_start(ov[:, bass.ds(t, 1), :], x_sb[:, bass.ds(t, 1), :]).then_inc(s_st, 16)
            sp.wait_ge(s_st, 16 * T)

        @block.tensor
        def _(pe):
            def split_mm(dst, lhi, llo, rhi, rlo, start, stop):
                pe.matmul(dst, lhi, rhi, start=start, stop=False)
                pe.matmul(dst, lhi, rlo, start=False, stop=False)
                return pe.matmul(dst, llo, rhi, start=False, stop=stop)

            def project(ch):
                n = slice(ch * CH, (ch + 1) * CH)
                pe.matmul(bank[QK[ch][1]][:, :], wqk_sb[:, 1, :], ctx_sb[:, n], start=True, stop=True).then_inc(s_k, 1)
                pe.matmul(bank[QK[ch][0]][:, :], wqk_sb[:, 0, :], ctx_sb[:, n], start=True, stop=True).then_inc(s_q, 1)

            def energy(b):
                for t in range(TB):
                    m = b * L + t * P
                    i = pe.matmul(bank[ENERGY[b]][:, t * L:(t + 1) * L], qT[:, m:m + P], kT[:, b * L:(b + 1) * L],
                                  start=True, stop=True)
                i.then_inc(s_e, 1)

            def transpose_batch(b, src, dst_bank, done):
                for k in range(KD):
                    for t in range(TB):
                        i = pe.transpose(dst_bank[:, k * L + t * P:k * L + (t + 1) * P],
                                         src[:, b * TB + t, k * P:(k + 1) * P], ident)
                i.then_inc(done, 1)

            def att_transpose(b):
                pe.wait_ge(s_att[b // BC], TB * (b % BC + 1))
                transpose_batch(b, att, bank[ENERGY[b]], s_attT)

            def mix(b):
                pe.wait_ge(s_attTc, b + 1)
                if b % BC == 0:
                    pe.wait_ge(ld[f"xT{b // BC}"], 16)
                for t in range(TB):
                    n = b * L + t * P
                    for k in range(KD):
                        i = pe.matmul(bank[MIX[b]][:, t * L:(t + 1) * L], xT_sb[:, k, n:n + P],
                                      attT[:, b, k, :], start=(k == 0), stop=(k == KD - 1))
                i.then_inc(s_xm, 1)

            def xh2_transpose(b):
                pe.wait_ge(s_xh2, b + 1)
                transpose_batch(b, xh2, bank[XH2T[b]], s_x2T)

            def logits(b):
                if b == 0:
                    pe.wait_ge(s_mglo, 1)
                pe.wait_ge(s_x2lo, b + 1)
                for t in range(TB):
                    n = (b % BC) * TB + t
                    m = slice(b * L + t * P, b * L + (t + 1) * P)
                    dst = bank[ROUTE][:, n * E:(n + 1) * E]
                    for k in range(KD):
                        pe.matmul(dst, xT_lo[:, k, m], gw_lo[:, k, :], start=(k == 0), stop=False)
                        i = split_mm(dst, xT_hi[:, k, m], xT_lo[:, k, m], gw_hi[:, k, :], gw_lo[:, k, :],
                                     False, k == KD - 1)
                i.then_inc(s_lg, 1)

            def we_transpose(ch):
                pe.wait_ge(s_we, ch + 1)
                for t in range(TC):
                    i = pe.transpose(bank[ROUTE_T][0:E, t * P:(t + 1) * P], we[:, ch * TC + t, :], ident)
                i.then_inc(s_weT, 1)

            def gather(ch):
                if ch == 0:
                    pe.wait_ge(s_onehot, 1)
                pe.wait_ge(s_weTc, ch + 1)
                for t in range(TC):
                    i = pe.matmul(bank[ROUTE][:, t * E:(t + 1) * E],
                                  weT[:, ch * CH + t * P:ch * CH + (t + 1) * P], onehot[:, :],
                                  start=True, stop=True)
                i.then_inc(s_fl, 1)

            def stack_transpose(ch):
                if ch == 0:
                    pe.wait_ge(s_id16, 1)
                pe.wait_ge(s_stk, ch + 1)
                dst = bank[ROUTE_T][:, :].bitcast(F16)
                for t in range(TC):
                    for s in range(2):
                        i = pe.transpose(dst[:, s * CH + t * P:s * CH + (t + 1) * P], stk[:, ch * TC + t, s, :],
                                         id16[:, :])
                i.then_inc(s_stT, 1)

            def scalar_transpose(ch):
                pe.wait_ge(s_sc, ch + 1)
                for t in range(TC):
                    i = pe.transpose(bank[ROUTE][0:G, t * P:(t + 1) * P], scal[:, ch * TC + t, :], ident)
                i.then_inc(s_scT, 1)

            def mu_block(n):
                w, s, groups = MU[n]
                if n == 0:
                    pe.wait_ge(s_pad, 2)
                    pe.wait_ge(s_qc, 1)
                    pe.wait_ge(s_kc, 1)
                pe.wait_ge(s_wlo[w][s], KD)
                if n >= 2:
                    pe.wait_ge(s_mu, n - 1)
                for slot, a, z in groups:
                    dst = bank[MU_BANK[n % 2]][:, a - groups[0][1]:z - groups[0][1]]
                    for k in range(KD):
                        i = split_mm(dst, pad_window(pad_hi, k, s, slot), pad_window(pad_lo, k, s, slot),
                                     w_hi[w][:, k, a:z], w_lo[w][:, k, a:z], k == 0, k == KD - 1)
                i.then_inc(s_mup, 1)

            def tile_x(ch, w, c, par, used, batch=None):
                if used is not None:
                    pe.wait_ge((s_silu, s_a)[w], used)
                first, last = (0, CH) if batch is None else (batch * L, (batch + 1) * L)
                n, col = slice(ch * CH + first, ch * CH + last), bass.ds(c * P, P)
                for k in range(KD):
                    split_mm(bank[(GATE, UP)[w][par]][:, first:last], w_hi[w][:, k, col], w_lo[w][:, k, col],
                             xT_hi[:, k, n], xT_lo[:, k, n],
                             k == 0 and batch != 1, False)

            def tile_soft(ch, w, c, s, par):
                n, col = slice(ch * CH, (ch + 1) * CH), bass.ds(c * P, P)
                pe.matmul(bank[(GATE, UP)[w][par]][:, :], mu[:, w, col], stkT[:, s, n],
                          start=False, stop=True).then_inc((s_g, s_u)[w], 1)

            def unit(ch, c, s, par, used):
                for w in range(2):
                    tile_x(ch, w, c, par, used)
                    tile_soft(ch, w, c, s, par)

            pe.wait_ge(s_warm, 1)
            for _ in range(WARM_UP):
                pe.matmul(bank[7][:, 0:P], warm[:, :], warm[:, :], start=True, stop=True)
            pe.wait_ge(ld["wqk"], 16)
            pe.wait_ge(ld["ctx0"], 16)
            project(0)
            pe.wait_ge(s_kc, 1)
            pe.wait_ge(s_qc, 1)
            energy(0)
            energy(1)
            pe.wait_ge(ld["ctx1"], 16)
            project(1)
            pe.wait_ge(ld["cst"], 16)
            att_transpose(0)
            att_transpose(1)
            mix(0)
            mix(1)
            pe.wait_ge(s_kc, 2)
            pe.wait_ge(s_qc, 2)
            energy(2)
            energy(3)
            mu_block(0)
            xh2_transpose(0)
            mu_block(1)
            xh2_transpose(1)
            logits(0)
            tile_x(0, 0, 0, 0, None, batch=0)
            logits(1)
            tile_x(0, 0, 0, 0, None, batch=1)
            pe.wait_ge(s_wlo[1][0], KD)
            tile_x(0, 1, 0, 0, None)
            mu_block(2)
            we_transpose(0)
            att_transpose(2)
            att_transpose(3)
            gather(0)
            mu_block(3)
            mu_block(4)
            mix(2)
            mu_block(5)
            scalar_transpose(0)
            mix(3)
            mu_block(6)
            stack_transpose(0)
            mu_block(7)
            pe.wait_ge(s_stTc, 1)
            tile_soft(0, 0, 0, 0, 0)
            tile_soft(0, 1, 0, 0, 0)
            pe.wait_ge(s_x1, 3)
            tile_x(0, 0, 1, 1, None)
            pe.wait_ge(s_mu, len(MU))
            tile_soft(0, 0, 1, 0, 1)
            pe.wait_ge(s_x1, 4)
            tile_x(0, 1, 1, 1, None)
            tile_soft(0, 1, 1, 0, 1)

            for c in range(1, NJ):
                if c >= 2:
                    unit(0, c, int(c >= SPLIT), c % 2, c - 1)
                if c == 1:
                    pe.wait_ge(s_scTc, 1)
                    xh2_transpose(2)
                    xh2_transpose(3)
                elif c == 2:
                    logits(2)
                    logits(3)
                elif c == 5:
                    we_transpose(1)
                elif c == 6:
                    gather(1)
                elif c == 8:
                    scalar_transpose(1)
                elif c == 9:
                    stack_transpose(1)
            pe.wait_ge(s_stTc, 2)
            for s, first, last in ((0, 0, SPLIT // 2), (1, SPLIT // 2, NJ // 2)):
                with pe.Fori(first, last) as i:
                    for h in range(2):
                        unit(1, 2 * i + h, s, (NJ + h) % 2, NJ + 2 * i + h - 1)
            unit(1, NJ - 1, 1, (2 * NJ - 1) % 2, 2 * NJ - 2)

            def down_tile(t, h, used):
                if used is not None:
                    pe.wait_ge(s_out, used)
                tok = bass.ds(t * P, P)
                for c in range(NJ):
                    y = split_mm(bank[6 + h][:, 0:D], a_hi[:, c, tok], a_lo[:, c, tok],
                                 down_hl[:, c, 0, :], down_hl[:, c, 1, :], c == 0, c == NJ - 1)
                y.then_inc(s_y, 1)

            pe.wait_ge(s_dhi, len(DOWN_PIECES))
            pe.wait_ge(s_dlo, len(DOWN_PIECES))
            pe.wait_ge(s_ahi, NJ)
            pe.wait_ge(s_alo, NJ)
            down_tile(0, 0, None)
            down_tile(1, 1, None)
            with pe.Fori(1, TC // 2) as i:
                for h in range(2):
                    down_tile(2 * i + h, h, 2 * i + h - 1)
            pe.wait_ge(s_ahi, NCH * NJ)
            pe.wait_ge(s_alo, NCH * NJ)
            with pe.Fori(TC // 2, T // 2) as i:
                for h in range(2):
                    down_tile(2 * i + h, h, 2 * i + h - 1)

        @block.scalar
        def _(act):
            act.dma_start(ctx_sb[:, 0:CH], ctxT[:, 0:CH]).then_inc(ld["ctx0"], 16)
            act.dma_start(bqk_sb[:, :], bqk).then_inc(ld["bqk"], 16)

            def q_copy(ch):
                act.wait_ge(s_q, ch + 1)
                act.activation(qT[:, ch * CH:(ch + 1) * CH], bank[QK[ch][0]][:, :], ACT.Identity,
                               bias=bqk_sb[:, 0:1]).then_inc(s_qc, 1)

            def exps(b):
                act.wait_ge(s_rmax, b + 1)
                for t in range(b * TB, (b + 1) * TB):
                    act.activation(att[:, t, :], bank[ENERGY[b]][:, (t % TB) * L:(t % TB + 1) * L], ACT.Exp,
                                   bias=rmax[:, t:t + 1], accum_out=rsum[:, t:t + 1]).then_inc(s_exp, 1)

            def attT_copy(b):
                act.wait_ge(s_attT, b + 1)
                act.copy(attT[:, b, :, :].rearrange("p k m -> p (k m)"), bank[ENERGY[b]][:, :]).then_inc(s_attTc, 1)

            def shift_x(b):
                if b % BC == 0:
                    act.wait_ge(s_shift, b // BC + 1)
                for t in range(b * TB, (b + 1) * TB):
                    i = act.activation(x_sb[:, t, :], x_sb[:, t, :], ACT.Identity, bias=shift1[:, t:t + 1])
                i.then_inc(s_xc, 1)

            def x2_hi(b):
                act.wait_ge(s_x2T, b + 1)
                act.copy(xT_hi[:, :, b * L:(b + 1) * L],
                         bank[XH2T[b]][:, :].rearrange("p (k n) -> p k n", k=KD)).then_inc(s_x2hi, 1)

            def logit_exps(ch):
                act.wait_ge(s_lmax, ch + 1)
                for t in range(TC):
                    n = ch * TC + t
                    act.activation(score[:, n, :], bank[ROUTE][:, t * E:(t + 1) * E], ACT.Exp,
                                   bias=lmax[:, n:n + 1], accum_out=lsum[:, n:n + 1]).then_inc(s_lexp, 1)

            def weT_copy(ch):
                act.wait_ge(s_weT, ch + 1)
                act.copy(weT[:, ch * CH:(ch + 1) * CH], bank[ROUTE_T][0:E, :]).then_inc(s_weTc, 1)

            def flat_exp(ch):
                act.wait_ge(s_fl, ch + 1)
                act.activation(fexp[:, ch * TC:(ch + 1) * TC, :].rearrange("p t e -> p (t e)"),
                               bank[ROUTE][:, 0:TC * E], ACT.Exp).then_inc(s_fexp, 1)

            def stack_copy(ch):
                act.wait_ge(s_stT, ch + 1)
                act.copy(stkT[:, :, ch * CH:(ch + 1) * CH],
                         bank[ROUTE_T][:, :].bitcast(F16).rearrange("p (s n) -> p s n", s=2)).then_inc(s_stTc, 1)

            def scalar_copy(ch):
                act.wait_ge(s_scT, ch + 1)
                act.copy(scalT[:, ch * CH:(ch + 1) * CH], bank[ROUTE][0:G, :]).then_inc(s_scTc, 1)

            def weight_hi(w, piece):
                act.wait_ge(ld[f"{('gate', 'up')[w]}{piece}"], 16)
                cols = (slice(0, EDGE), slice(EDGE, GI))[piece]
                act.copy(w_hi[w][:, :, cols], w32[w][:, :, cols]).then_inc(s_whi[w], 1)

            def down_hi(n):
                c = slice(*DOWN_PIECES[n])
                act.copy(down_hl[:, c, 0, :], down32[:, c, :]).then_inc(s_dhi, 1)

            def mu_high(n):
                cols = MU[n][2][-1][2] - MU[n][2][0][1]
                act.wait_ge(s_mup, n + 1)
                if n >= 2:
                    act.wait_ge(s_mu, n - 1)
                act.copy(mu_hi[:, n % 2, 0:cols], bank[MU_BANK[n % 2]][:, 0:cols]).then_inc(s_muhi, 1)

            def gate_silu(n, par, used):
                act.wait_ge(s_g, n + 1)
                if used is not None:
                    act.wait_ge(s_a, used)
                act.activation(silu[:, par, :], bank[GATE[par]][:, :], ACT.Silu).then_inc(s_silu, 1)

            def activation_high(n, c, par, tok):
                act.wait_ge(s_a, n + 1)
                act.copy(a_hi[:, c, tok], act32[:, par, :]).then_inc(s_ahi, 1)

            def activate(n, c, par, tok, used):
                gate_silu(n, par, used)
                activation_high(n, c, par, tok)

            act.wait_ge(s_warm, 1)
            act.activation(unused[:, :], warm[:, 0:2], ACT.Tanh)
            act.wait_ge(ld["gates"], 16)
            act.activation(tg[:, :], gates_sb[:, :], ACT.Tanh).then_inc(s_tg, 1)
            act.wait_ge(ld["mg"], 16)
            act.copy(mg_hi[:, :, :], mg32[:, :, :]).then_inc(s_mghi, 1)
            act.wait_ge(ld["bqk"], 16)
            q_copy(0)
            weight_hi(0, 0)
            exps(0)
            exps(1)
            attT_copy(0)
            attT_copy(1)
            q_copy(1)
            shift_x(0)
            weight_hi(1, 0)
            shift_x(1)
            weight_hi(0, 1)
            act.wait_ge(ld["cst"], 16)
            act.copy(id16[:, :], ident).then_inc(s_id16, 1)
            weight_hi(1, 1)
            x2_hi(0)
            exps(2)
            x2_hi(1)
            mu_high(0)
            exps(3)
            mu_high(1)
            logit_exps(0)
            mu_high(2)
            weT_copy(0)
            attT_copy(2)
            attT_copy(3)
            flat_exp(0)
            mu_high(3)
            mu_high(4)
            shift_x(2)
            mu_high(5)
            scalar_copy(0)
            shift_x(3)
            mu_high(6)
            stack_copy(0)
            mu_high(7)
            for c in range(NJ):
                gate_silu(c, c % 2, c - 1 if c >= 2 else None)
                if c == 1:
                    x2_hi(2)
                    x2_hi(3)
                elif c == 3:
                    logit_exps(1)
                elif c == 5:
                    weT_copy(1)
                elif c == 7:
                    flat_exp(1)
                elif c == 9:
                    scalar_copy(1)
                elif c == 10:
                    stack_copy(1)
                activation_high(c, c, c % 2, slice(0, CH))
                if c % 2 == 0 and c // 2 < len(DOWN_PIECES):
                    if c == 0:
                        act.wait_ge(ld["down"], 16)
                    down_hi(c // 2)
            tok1 = slice(CH, 2 * CH)
            with act.Fori(0, NJ // 2) as i:
                for h in range(2):
                    n = 2 * i + (NJ + h)
                    activate(n, bass.ds(2 * i + h, 1), (NJ + h) % 2, tok1, n - 1)
            activate(2 * NJ - 1, NJ - 1, (2 * NJ - 1) % 2, tok1, 2 * NJ - 2)

        @block.gpsimd
        def _(pool):
            def clear(tile):
                return pool.memset(tile.bitcast(F32) if tile.dtype == F16 else tile, 0.0)

            def reciprocal_root(var, rstd, src, b, batches, ready, done):
                r = slice(b * TB, (b + batches) * TB)
                pool.wait_ge(ready, b + batches)
                step(pool.tensor_scalar(var[:, r], src[:, r, 1], EPS, None, ALU.add))
                pool.tensor_tensor(rstd[:, r], var[:, r], half[:, 0:batches * TB], ALU.pow).then_inc(done, batches)

            steps = [0]

            def step(instruction):
                steps[0] += 1
                instruction.then_inc(pool_step, 1)
                pool.wait_ge(pool_step, steps[0])

            def weight_lo(w, piece, k):
                pool.wait_ge(s_whi[w], piece + 1)
                cols = (slice(0, EDGE), slice(EDGE, GI))[piece]
                pool.tensor_tensor(w_lo[w][:, k, cols], w32[w][:, k, cols], w_hi[w][:, k, cols],
                                   ALU.subtract).then_inc(s_wlo[w][piece], 1)

            def shifts(ch):
                r = slice(ch * TC, (ch + 1) * TC)
                reciprocal_root(var1, rstd1, mv, ch * BC, BC, s_mv1, s_rstd1)
                pool.wait_ge(s_rstd1, BC * (ch + 1))
                step(pool.tensor_tensor(mr1[:, r], rstd1[:, r], mv[:, r, 0], ALU.mult))
                if ch == 0:
                    pool.wait_ge(s_tg, 1)
                pool.tensor_scalar(shift1[:, r], mr1[:, r], tg[:, 0:1], -1.0, ALU.mult, ALU.mult
                                   ).then_inc(s_shift, 1)

            def scale_att(b):
                pool.wait_ge(s_rinv, b + 1)
                for t in range(b * TB, (b + 1) * TB):
                    pool.tensor_scalar(att[:, t, :], att[:, t, :], rinv[:, t:t + 1], tg[:, 0:1],
                                       ALU.mult, ALU.mult).then_inc(s_att[b // BC], 1)

            def activation_low(n, c, par, tok):
                pool.wait_ge(s_ahi, n + 1)
                pool.tensor_tensor(a_lo[:, c, tok], act32[:, par, :], a_hi[:, c, tok],
                                   ALU.subtract).then_inc(s_alo, 1)

            step(pool.memset(half[:, :], -0.5))
            clear(pad_hi[:, :, :, :].rearrange("p k s w -> p (k s w)"))
            step(clear(pad_lo[:, :, :, :].rearrange("p k s w -> p (k s w)")))
            pool.memset(stk[:, :, :, 3 * COPY:], 0.0).then_inc(s_stk0, 1)
            pool.wait_ge(s_mghi, 1)
            pool.tensor_tensor(mg_lo[:, :, :], mg32[:, :, :], mg_hi[:, :, :], ALU.subtract).then_inc(s_mglo, 1)
            pool.wait_ge(s_mglo, 1)
            for pad, mask in ((pad_hi, mask_hi), (pad_lo, mask_lo)):
                for s, first in ((0, 0), (1, 1)):
                    for k in range(KD):
                        g0 = BASE[s] + first
                        dst = pad[:, k, s, :].rearrange("p (g w) -> p g w", w=P)[:, first:SG, 0:3 * COPY]
                        dst = dst.rearrange("p g (r c) -> p g r c", r=3)[:, :, :, 0:GS]
                        src = mask[:, k, g0 * GS:(g0 + SG - first) * GS].rearrange("p (g a i) -> p g a i", a=1, i=GS)
                        i = pool.tensor_copy(dst, src.to_broadcast([P, SG - first, 3, GS]))
                i.then_inc(s_pad, 1)
            shifts(0)
            pool.wait_ge(ld["inv"], 16)
            step(pool.tensor_copy(inv_f[:, :], inv_i[:, :]))
            step(pool.tensor_scalar(inv_n[:, :], inv_f[:, :], 0.0, float(E), ALU.is_lt, ALU.mult))
            step(pool.tensor_tensor(inv_f[:, :], inv_f[:, :], inv_n[:, :], ALU.add))
            step(pool.tensor_scalar(inv_f[:, :], inv_f[:, :], 0.0, float(E - 1), ALU.max, ALU.min))
            pool.wait_ge(ld["cst"], 16)
            pool.tensor_scalar(onehot[:, :], inv_f[:, :], cst[0:E, K_IOTA:K_IOTA + 1], None,
                               ALU.is_equal).then_inc(s_onehot, 1)
            reciprocal_root(var2, rstd2, mv2, 0, 1, s_mv2, s_rstd2)
            reciprocal_root(var2, rstd2, mv2, 1, 1, s_mv2, s_rstd2)
            weight_lo(1, 0, 0)
            scale_att(2)
            weight_lo(1, 0, 1)
            scale_att(3)
            weight_lo(0, 1, 0)
            weight_lo(0, 1, 1)
            weight_lo(1, 1, 0)
            weight_lo(1, 1, 1)
            shifts(1)
            for c in range(NJ):
                if c == 0:
                    reciprocal_root(var2, rstd2, mv2, 2, 2, s_mv2, s_rstd2)
                activation_low(c, c, c % 2, slice(0, CH))
                if c % 2 and c // 2 < len(DOWN_PIECES):
                    n = c // 2
                    pool.wait_ge(s_dhi, n + 1)
                    d = slice(*DOWN_PIECES[n])
                    pool.tensor_tensor(down_hl[:, d, 1, :], down32[:, d, :], down_hl[:, d, 0, :],
                                       ALU.subtract).then_inc(s_dlo, 1)
            tok1 = slice(CH, 2 * CH)
            with pool.Fori(0, NJ // 2) as i:
                for h in range(2):
                    activation_low(2 * i + (NJ + h), bass.ds(2 * i + h, 1), (NJ + h) % 2, tok1)
            activation_low(2 * NJ - 1, NJ - 1, (2 * NJ - 1) % 2, tok1)

        @block.vector
        def _(dve):
            steps = [0]

            def step(instruction):
                steps[0] += 1
                instruction.then_inc(dve_step, 1)
                dve.wait_ge(dve_step, steps[0])

            def statistics(mean_var, stat, b, done):
                tiles = range(b * TB, (b + 1) * TB)
                for t in tiles:
                    i = dve.bn_stats(stat[:, t % TC, :], x_sb[:, t, :])
                step(i)
                for t in tiles:
                    i = dve.bn_aggr(mean_var[:, t, :], stat[:, t % TC, :])
                i.then_inc(done, 1)

            def statistics1(b):
                dve.wait_ge(ld[f"x{b // BC}"], 16)
                statistics(mv, stats, b, s_mv1)

            def k_copy(ch):
                dve.wait_ge(s_k, ch + 1)
                dve.tensor_scalar(kT[:, ch * CH:(ch + 1) * CH], bank[QK[ch][1]][:, :], bqk_sb[:, 1:2], None,
                                  ALU.add).then_inc(s_kc, 1)

            def row_max(b):
                dve.wait_ge(s_e, b + 1)
                dve.tensor_reduce(rmax[:, b * TB:(b + 1) * TB],
                                  bank[ENERGY[b]][:, :].rearrange("p (t n) -> p t n", t=TB), AX.X, ALU.max,
                                  negate=True).then_inc(s_rmax, 1)

            def sum_reciprocal(b):
                dve.wait_ge(s_exp, (b + 1) * TB)
                dve.reciprocal(rinv[:, b * TB:(b + 1) * TB], rsum[:, b * TB:(b + 1) * TB]).then_inc(s_rinv, 1)

            def scale_att(b):
                sum_reciprocal(b)
                dve.wait_ge(s_rinv, b + 1)
                for t in range(b * TB, (b + 1) * TB):
                    dve.tensor_scalar(att[:, t, :], att[:, t, :], rinv[:, t:t + 1], tg[:, 0:1],
                                      ALU.mult, ALU.mult).then_inc(s_att[b // BC], 1)

            def residual(b):
                if b % BC == 0:
                    dve.wait_ge(s_rstd1, b + BC)
                dve.wait_ge(s_xc, b + 1)
                dve.wait_ge(s_xm, b + 1)
                for t in range(b * TB, (b + 1) * TB):
                    i = dve.scalar_tensor_tensor(x_sb[:, t, :], bank[MIX[b]][:, (t % TB) * L:(t % TB + 1) * L],
                                                 rstd1[:, t:t + 1], x_sb[:, t, :], ALU.mult, ALU.add)
                i.then_inc(s_x1, 1)

            def statistics2(b):
                dve.wait_ge(s_x1, b + 1)
                statistics(mv2, stats2, b, s_mv2)

            def normalise2(b):
                dve.wait_ge(s_rstd2, b + 1)
                for t in range(b * TB, (b + 1) * TB):
                    i = dve.tensor_scalar(xh2[:, t, :], x_sb[:, t, :], mv2[:, t, 0:1], rstd2[:, t:t + 1],
                                          ALU.subtract, ALU.mult)
                i.then_inc(s_xh2, 1)

            def x2_lo(b):
                dve.wait_ge(s_x2hi, b + 1)
                dve.tensor_tensor(xT_lo[:, :, b * L:(b + 1) * L],
                                  bank[XH2T[b]][:, :].rearrange("p (k n) -> p k n", k=KD),
                                  xT_hi[:, :, b * L:(b + 1) * L], ALU.subtract).then_inc(s_x2lo, 1)

            def logit_max(ch):
                dve.wait_ge(s_lg, BC * (ch + 1))
                dve.tensor_reduce(lmax[:, ch * TC:(ch + 1) * TC],
                                  bank[ROUTE][:, 0:TC * E].rearrange("p (t e) -> p t e", t=TC), AX.X, ALU.max,
                                  negate=True).then_inc(s_lmax, 1)

            def top_scores(ch):
                r, tiles = slice(ch * TC, (ch + 1) * TC), range(ch * TC, (ch + 1) * TC)
                dve.wait_ge(s_lexp, (ch + 1) * TC)
                step(dve.reciprocal(linv[:, r], lsum[:, r]))
                for t in tiles:
                    i = dve.tensor_scalar(score[:, t, :], score[:, t, :], linv[:, t:t + 1], None, ALU.mult)
                step(i)
                for t in tiles:
                    i = dve.max(top8[:, t, :], score[:, t, :])
                step(i)
                for t in tiles:
                    i = dve.match_replace(rest[:, t, :], top8[:, t, :], score[:, t, :], 0.0)
                step(i)
                dve.tensor_tensor(we[:, r, :], score[:, r, :], rest[:, r, :], ALU.subtract).then_inc(s_we, 1)

            def grouped(tile, r):
                return tile[:, r, :].rearrange("p t (g i) -> p (t g) i", i=GS)

            def slot_softmax(ch):
                r = slice(ch * TC, (ch + 1) * TC)
                flat = bank[ROUTE][:, 0:TC * E]

                def flattened(tile):
                    return tile[:, r, :].rearrange("p t e -> p (t e)")

                dve.wait_ge(s_fexp, ch + 1)
                step(dve.tensor_scalar(flattened(live), flat, 0.0, TINY, ALU.not_equal, ALU.max))
                dve.tensor_reduce(flattened(scal), flat.rearrange("p (g i) -> p g i", i=GS), AX.X, ALU.add
                                  ).then_inc(s_sc, 1)
                step(dve.tensor_tensor(fexp[:, r, :], fexp[:, r, :], live[:, r, :], ALU.mult))
                step(dve.tensor_reduce(flattened(den), grouped(fexp, r), AX.X, ALU.add))
                dve.reciprocal(dinv[:, r, :], den[:, r, :]).then_inc(s_dinv, 1)

            def make_stacks(ch):
                r = slice(ch * TC, (ch + 1) * TC)
                dve.wait_ge(s_dinv, ch + 1)
                step(dve.tensor_tensor(grouped(soft, r), grouped(fexp, r),
                                       dinv[:, r, :].rearrange("p t (g a) -> p (t g) a", a=1)
                                       .to_broadcast([P, TC * G, GS]), ALU.mult))
                if ch == 0:
                    dve.wait_ge(s_stk0, 1)
                for s in range(2):
                    src = soft[:, r, BASE[s] * GS:BASE[s] * GS + COPY]
                    dve.tensor_copy(stk[:, r, s, 0:COPY], src)
                    i = dve.tensor_copy(stk[:, r, s, COPY:2 * COPY], src)
                step(i)
                for s in range(2):
                    src = soft[:, r, BASE[s] * GS:BASE[s] * GS + COPY]
                    i = dve.tensor_tensor(stk[:, r, s, 2 * COPY:3 * COPY], src, stk[:, r, s, 0:COPY],
                                          ALU.subtract)
                i.then_inc(s_stk, 1)

            def weight_lo(w, piece, k):
                dve.wait_ge(s_whi[w], piece + 1)
                cols = (slice(0, EDGE), slice(EDGE, GI))[piece]
                dve.tensor_tensor(w_lo[w][:, k, cols], w32[w][:, k, cols], w_hi[w][:, k, cols],
                                  ALU.subtract).then_inc(s_wlo[w][piece], 1)

            def mu_stack(n):
                w, _, groups = MU[n]
                a, z = groups[0][1], groups[-1][2]
                dve.wait_ge(s_muhi, n + 1)
                dve.scalar_tensor_tensor(mu[:, w, a:z], mu_hi[:, n % 2, 0:z - a], neg_mu,
                                         bank[MU_BANK[n % 2]][:, 0:z - a], ALU.mult, ALU.add).then_inc(s_mu, 1)

            def multiply(n, par, rows, low):
                dve.wait_ge(s_silu, n + 1)
                dve.wait_ge(s_rows[par], 32 * rows)
                dve.tensor_tensor(silu[:, par, :], silu[:, par, :], scal_rows[:, par, :], ALU.mult
                                  ).then_inc(s_prod, 1)
                dve.wait_ge(s_prod, n + 1)
                dve.wait_ge(s_u, n + 1)
                if low is not None:
                    dve.wait_ge(s_ahi, low)
                    dve.wait_ge(s_alo, low)
                dve.tensor_tensor(act32[:, par, :], silu[:, par, :], bank[UP[par]][:, :], ALU.mult
                                  ).then_inc(s_a, 1)

            dve.memset(warm[:, :].bitcast(F32), 0.0).then_inc(s_warm, 1)
            dve.wait_ge(ld["bqk"], 16)
            k_copy(0)
            statistics1(0)
            statistics1(1)
            row_max(0)
            row_max(1)
            dve.wait_ge(s_tg, 1)
            scale_att(0)
            scale_att(1)
            k_copy(1)
            weight_lo(0, 0, 0)
            weight_lo(0, 0, 1)
            residual(0)
            statistics2(0)
            residual(1)
            statistics2(1)
            normalise2(0)
            row_max(2)
            normalise2(1)
            x2_lo(0)
            row_max(3)
            x2_lo(1)
            sum_reciprocal(2)
            mu_stack(0)
            logit_max(0)
            sum_reciprocal(3)
            mu_stack(1)
            top_scores(0)
            mu_stack(2)
            statistics1(2)
            statistics1(3)
            mu_stack(3)
            slot_softmax(0)
            mu_stack(4)
            residual(2)
            mu_stack(5)
            make_stacks(0)
            residual(3)
            mu_stack(6)
            statistics2(2)
            statistics2(3)
            mu_stack(7)
            for c in range(NJ):
                multiply(c, c % 2, c // 2 + 1, c - 1 if c >= 2 else None)
                if c in (0, 1):
                    for b in (2, 3):
                        (normalise2, x2_lo)[c](b)
                elif c == 2:
                    logit_max(1)
                elif c == 3:
                    top_scores(1)
                elif c == 7:
                    slot_softmax(1)
                elif c == 8:
                    make_stacks(1)
            with dve.Fori(0, NJ // 2) as i:
                for h in range(2):
                    n = 2 * i + (NJ + h)
                    multiply(n, (NJ + h) % 2, i + ((NJ + h) // 2 + 1), n - 1)
            multiply(2 * NJ - 1, (2 * NJ - 1) % 2, NJ, 2 * NJ - 2)

            with dve.Fori(0, T // 2) as i:
                for h in range(2):
                    t = 2 * i + h
                    row = x_sb[:, bass.ds(t, 1), :].rearrange("p t d -> p (t d)")
                    dve.wait_ge(s_y, t + 1)
                    dve.scalar_tensor_tensor(row, bank[6 + h][:, 0:D], tg[:, 1:2], row,
                                             ALU.mult, ALU.add).then_inc(s_out, 1)


_OUT = ((B, L, D), "float32")


def kernel(x, ctx_1024, g_xattn, g_ffn, L0_xattn_Wq, L0_xattn_bq, L0_xattn_Wk, L0_xattn_bk, L0_ffn_gate_w,
           L0_ffn_mask_up_w, L0_ffn_gate_proj_w, L0_ffn_up_proj_w, L0_ffn_down_proj_w, L0_ffn_inv_map):
    import concourse.bacc as bacc
    from concourse.bass_utils import run_bass_kernel_spmd

    inv = np.ascontiguousarray(L0_ffn_inv_map).reshape(-1)
    if inv.dtype.itemsize == 8:
        inv = inv.view(np.int32)[::2]
    arrays = {
        "ctxT": np.asarray(ctx_1024).reshape(B * L, C).T,
        "x": np.asarray(x),
        "xT": np.asarray(x).reshape(B * L, D).T,
        "wqkT": np.concatenate([np.asarray(L0_xattn_Wq).T, np.asarray(L0_xattn_Wk).T], 1),
        "bqk": np.stack([np.asarray(L0_xattn_bq), np.asarray(L0_xattn_bk)], 1),
        "gates": np.concatenate([np.asarray(g_xattn), np.asarray(g_ffn)]),
        "gateT": np.asarray(L0_ffn_gate_proj_w).reshape(GI, D).T,
        "upT": np.asarray(L0_ffn_up_proj_w).reshape(GI, D).T,
        "downT": np.asarray(L0_ffn_down_proj_w).transpose(0, 2, 1).reshape(GI, D),
        "maskgwT": np.concatenate([np.asarray(L0_ffn_mask_up_w).transpose(1, 0, 2).reshape(D, E),
                                   np.asarray(L0_ffn_gate_w).T], 1),
        "inv_map": inv,
        "consts": constants(),
    }
    arrays = {f"in_{k}": np.ascontiguousarray(v) for k, v in arrays.items()}
    nc = bacc.Bacc("TRN2", target_bir_lowering=False, num_devices=1)
    args = [nc.dram_tensor(k, v.shape, mybir.dt.from_np(v.dtype), kind="ExternalInput").ap()
            for k, v in arrays.items()]
    out = nc.dram_tensor("out", _OUT[0], mybir.dt.from_np(np.dtype(_OUT[1])), kind="ExternalOutput").ap()
    block_kernel(nc, *args, out)
    r = run_bass_kernel_spmd(nc, [arrays], core_ids=[0])
    return r.results[0]["out"]
```
